# Optimizing a Trainium2 kernel written in Bass

```python
import numpy as np
import jax
import jax.numpy as jnp

def _softmax(x, axis=-1):
    return jax.nn.softmax(x, axis=axis)

def _gelu(x):
    return jax.nn.gelu(x, approximate=True)

def _silu(x):
    return jax.nn.silu(x)

def _sigmoid(x):
    return jax.nn.sigmoid(x)

def _layernorm(x, axis=-1, eps=1e-05):
    m = jnp.mean(x, axis=axis, keepdims=True)
    v = jnp.var(x, axis=axis, keepdims=True)
    return (x - m) / jnp.sqrt(v + eps)

def _scatter_add(tgt, idx, src, axis=0):
    return tgt.at[idx].add(src)

def _segment_sum(src, seg, n):
    return jax.ops.segment_sum(src, seg, n)
kernel_name = 'mk_gps_d1_gnn_r8_6ba634'

def setup_inputs(seed: int=0):
    np.random.seed(seed)
    _w = jnp.asarray

    def _rec_inputs():
        import jax
        import jax.numpy as jnp
        _gk = jax.random.key(seed)
        x = -0.0003713 + 1 * jax.random.normal(jax.random.fold_in(_gk, 1), (6250, 256), jnp.float32)
        src = jax.random.randint(jax.random.fold_in(_gk, 2), (200000,), 0, 6250, jnp.int32)
        dst = jnp.minimum((6250 * jax.random.uniform(jax.random.fold_in(_gk, 3), (200000,)) ** 2.0).astype(jnp.int32), 49999)
        _o = jnp.argsort(dst, stable=True)
        src = src[_o]
        dst = dst[_o]
        return (x, src, dst)
    x, src, dst = _rec_inputs()

    def _L0_gnn_setup():
        import jax, jax.numpy as jnp
        import numpy as np
        N_NODES = 6250
        D = 256
        N_EDGES = 37500
        key = jax.random.key(seed)
        ks = jax.random.split(key, 6)
        s = 1.0 / np.sqrt(D)
        x = jax.random.normal(ks[0], (N_NODES, D), dtype=jnp.float32)
        edge_index = jax.random.randint(ks[1], (2, N_EDGES), 0, N_NODES, dtype=jnp.int64)
        W_l = jax.random.normal(ks[2], (D, D), dtype=jnp.float32) * s
        b_l = jnp.zeros((D,), dtype=jnp.float32)
        W_r = jax.random.normal(ks[3], (D, D), dtype=jnp.float32) * s
        W_ln = jax.random.normal(ks[4], (D, D), dtype=jnp.float32) * s
        return {'x': x, 'edge_index': edge_index, 'W_l': W_l, 'b_l': b_l, 'W_r': W_r, 'W_ln': W_ln}
    _L0_gnn_all = _L0_gnn_setup()
    _L0_gnn_in = {k: v for k, v in _L0_gnn_all.items() if k in ('W_l', 'b_l', 'W_r', 'W_ln')}
    del _L0_gnn_all

    def _L0_mix_setup():
        import jax, jax.numpy as jnp
        import numpy as np
        MIDC = 256
        HEADS = 8
        HEADC = MIDC // HEADS
        EPS = 1e-05

        def _ln(x, gamma, beta):
            mu = jnp.mean(x, axis=-1, keepdims=True)
            var = jnp.var(x, axis=-1, keepdims=True)
            return (x - mu) * jax.lax.rsqrt(var + EPS) * gamma + beta
        key = jax.random.key(seed)
        ks = jax.random.split(key, 8)
        B, HW, C = (8, 512, MIDC)
        s = 1.0 / np.sqrt(C)
        return {'x': jax.random.normal(ks[0], (B, HW, C), jnp.float32), 'w_qkv': jax.random.normal(ks[1], (C, 3 * C), jnp.float32) * s, 'b_qkv': jnp.zeros((3 * C,), jnp.float32), 'kln_g': jnp.ones((HEADC,), jnp.float32), 'kln_b': jnp.zeros((HEADC,), jnp.float32), 'vln_g': jnp.ones((HEADC,), jnp.float32), 'vln_b': jnp.zeros((HEADC,), jnp.float32), 'w1': jax.random.normal(ks[2], (C, C), jnp.float32) * s, 'b1': jnp.zeros((C,), jnp.float32), 'w2': jax.random.normal(ks[3], (C, C), jnp.float32) * s, 'b2': jnp.zeros((C,), jnp.float32)}
    _L0_mix_all = _L0_mix_setup()
    _L0_mix_in = {k: v for k, v in _L0_mix_all.items() if k in ('w_qkv', 'b_qkv', 'kln_g', 'kln_b', 'vln_g', 'vln_b', 'w1', 'b1', 'w2', 'b2')}
    del _L0_mix_all

    def _L0_ffn_setup():
        import jax, jax.numpy as jnp
        import numpy as np
        B, S, D, F, E, K = (8, 256, 256, 1024, 8, 2)
        key = jax.random.key(seed)
        ks = jax.random.split(key, 10)
        s = 0.02
        return {'x': jax.random.normal(ks[0], (B, S, D), dtype=jnp.float32), 'Wr': jax.random.normal(ks[1], (D, E), dtype=jnp.float32) * s, 'W1s': jax.random.normal(ks[2], (D, F), dtype=jnp.float32) * s, 'b1s': jnp.zeros((F,), dtype=jnp.float32), 'W2s': jax.random.normal(ks[3], (F, D), dtype=jnp.float32) * s, 'b2s': jnp.zeros((D,), dtype=jnp.float32), 'W1p': jax.random.normal(ks[4], (E, D, F), dtype=jnp.float32) * s, 'b1p': jnp.zeros((E, F), dtype=jnp.float32), 'W2p': jax.random.normal(ks[5], (E, F, D), dtype=jnp.float32) * s, 'b2p': jnp.zeros((E, D), dtype=jnp.float32)}
    _L0_ffn_all = _L0_ffn_setup()
    _L0_ffn_in = {k: v for k, v in _L0_ffn_all.items() if k in ('Wr', 'W1s', 'b1s', 'W2s', 'b2s', 'W1p', 'b1p', 'W2p', 'b2p')}
    del _L0_ffn_all
    return {'x': x, 'src': src, 'dst': dst, 'L0_gnn_W_l': _L0_gnn_in['W_l'], 'L0_gnn_b_l': _L0_gnn_in['b_l'], 'L0_gnn_W_r': _L0_gnn_in['W_r'], 'L0_gnn_W_ln': _L0_gnn_in['W_ln'], 'L0_mix_w_qkv': _L0_mix_in['w_qkv'], 'L0_mix_b_qkv': _L0_mix_in['b_qkv'], 'L0_mix_kln_g': _L0_mix_in['kln_g'], 'L0_mix_kln_b': _L0_mix_in['kln_b'], 'L0_mix_vln_g': _L0_mix_in['vln_g'], 'L0_mix_vln_b': _L0_mix_in['vln_b'], 'L0_mix_w1': _L0_mix_in['w1'], 'L0_mix_b1': _L0_mix_in['b1'], 'L0_mix_w2': _L0_mix_in['w2'], 'L0_mix_b2': _L0_mix_in['b2'], 'L0_ffn_Wr': _L0_ffn_in['Wr'], 'L0_ffn_W1s': _L0_ffn_in['W1s'], 'L0_ffn_b1s': _L0_ffn_in['b1s'], 'L0_ffn_W2s': _L0_ffn_in['W2s'], 'L0_ffn_b2s': _L0_ffn_in['b2s'], 'L0_ffn_W1p': _L0_ffn_in['W1p'], 'L0_ffn_b1p': _L0_ffn_in['b1p'], 'L0_ffn_W2p': _L0_ffn_in['W2p'], 'L0_ffn_b2p': _L0_ffn_in['b2p']}

def reference(x, src, dst, L0_gnn_W_l, L0_gnn_b_l, L0_gnn_W_r, L0_gnn_W_ln, L0_mix_w_qkv, L0_mix_b_qkv, L0_mix_kln_g, L0_mix_kln_b, L0_mix_vln_g, L0_mix_vln_b, L0_mix_w1, L0_mix_b1, L0_mix_w2, L0_mix_b2, L0_ffn_Wr, L0_ffn_W1s, L0_ffn_b1s, L0_ffn_W2s, L0_ffn_b2s, L0_ffn_W1p, L0_ffn_b1p, L0_ffn_W2p, L0_ffn_b2p):
    import jax
    import jax.numpy as jnp

    def _L0_gnn_ref(x, edge_index, W_l, b_l, W_r, W_ln):
        import jax, jax.numpy as jnp
        import numpy as np
        N_NODES = 6250
        D = 256
        N_EDGES = 37500
        n = x.shape[0]
        src = edge_index[0]
        dst = edge_index[1]
        msg_sum = jax.ops.segment_sum(x[src], dst, num_segments=n)
        cnt = jax.ops.segment_sum(jnp.ones_like(dst, dtype=x.dtype), dst, num_segments=n)
        mean = msg_sum / jnp.maximum(cnt, 1.0)[:, None]
        sage = mean @ W_l.T + b_l + x @ W_r.T
        out = jax.nn.relu(sage)
        out = out @ W_ln.T
        out = out + x
        return jax.nn.relu(out)

    def _L0_mix_ref(x, w_qkv, b_qkv, kln_g, kln_b, vln_g, vln_b, w1, b1, w2, b2):
        import jax, jax.numpy as jnp
        import numpy as np
        MIDC = 256
        HEADS = 8
        HEADC = MIDC // HEADS
        EPS = 1e-05

        def _ln(x, gamma, beta):
            mu = jnp.mean(x, axis=-1, keepdims=True)
            var = jnp.var(x, axis=-1, keepdims=True)
            return (x - mu) * jax.lax.rsqrt(var + EPS) * gamma + beta
        B, HW, C = x.shape
        bias = x
        qkv = (x @ w_qkv + b_qkv).reshape(B, HW, HEADS, 3 * HEADC)
        qkv = qkv.transpose(0, 2, 1, 3)
        q, k, v = jnp.split(qkv, 3, axis=-1)
        k = _ln(k, kln_g, kln_b)
        v = _ln(v, vln_g, vln_b)
        kv = jnp.einsum('bhnd,bhne->bhde', k, v) / HW
        out = jnp.einsum('bhnd,bhde->bhne', q, kv)
        out = out.transpose(0, 2, 1, 3).reshape(B, HW, C)
        ret = out + bias
        h = jax.nn.gelu(ret @ w1 + b1, approximate=False)
        return h @ w2 + b2 + bias

    def _L0_ffn_ref(x, Wr, W1s, b1s, W2s, b2s, W1p, b1p, W2p, b2p):
        import jax, jax.numpy as jnp
        import numpy as np
        B, S, D, F, E, K = (8, 256, 256, 1024, 8, 2)
        gelu = lambda t: jax.nn.gelu(t, approximate=False)
        shared = gelu(x @ W1s + b1s) @ W2s + b2s
        rw = jax.nn.softmax(x @ Wr, axis=-1)
        topw, topi = jax.lax.top_k(rw, K)
        topw = topw / jnp.sum(topw, axis=-1, keepdims=True)
        mask = jnp.sum(jax.nn.one_hot(topi, E, dtype=topw.dtype) * topw[..., None], axis=-2)
        h = gelu(jnp.einsum('bsd,edf->bsef', x, W1p) + b1p)
        priv = jnp.einsum('bsef,efd->bsed', h, W2p) + b2p
        routed = jnp.einsum('bsed,bse->bsd', priv, mask)
        return shared + routed
    edge_index = jnp.stack([src, dst])
    xn = _layernorm(x, axis=-1)
    x = x + _L0_gnn_ref(xn, edge_index, L0_gnn_W_l, L0_gnn_b_l, L0_gnn_W_r, L0_gnn_W_ln) + _L0_mix_ref(xn[None], L0_mix_w_qkv, L0_mix_b_qkv, L0_mix_kln_g, L0_mix_kln_b, L0_mix_vln_g, L0_mix_vln_b, L0_mix_w1, L0_mix_b1, L0_mix_w2, L0_mix_b2)[0]
    x = x + _L0_ffn_ref(_layernorm(x, axis=-1)[None], L0_ffn_Wr, L0_ffn_W1s, L0_ffn_b1s, L0_ffn_W2s, L0_ffn_b2s, L0_ffn_W1p, L0_ffn_b1p, L0_ffn_W2p, L0_ffn_b2p)[0]
    return x

_drawn_inputs = setup_inputs


def setup_inputs(seed=0):
    import zlib

    import numpy as np

    out = dict(_drawn_inputs(seed))
    spreads = {'L0_gnn_b_l': (0.0, 0.393),
     'L0_mix_b_qkv': (0.0, 0.322),
     'L0_mix_kln_g': (1.0, 0.6),
     'L0_mix_kln_b': (0.0, 0.534),
     'L0_mix_vln_g': (1.0, 0.6),
     'L0_mix_vln_b': (0.0, 0.479),
     'L0_mix_b1': (0.0, 0.318),
     'L0_mix_b2': (0.0, 0.1),
     'L0_ffn_b1s': (0.0, 0.665),
     'L0_ffn_b2s': (0.0, 0.1),
     'L0_ffn_b1p': (0.0, 0.8),
     'L0_ffn_b2p': (0.0, 0.299)}
    factors = {}
    for name, (base, spread) in spreads.items():
        noise = np.random.default_rng([zlib.crc32(name.encode()), seed]).standard_normal(out[name].shape)
        drawn = base * np.exp(spread * noise) if base else spread * noise
        out[name] = jnp.asarray(drawn.astype(out[name].dtype))
    for name, factor in factors.items():
        out[name] = (out[name] * factor).astype(out[name].dtype)
    return out
```

```python
import concourse.bass as bass
from concourse import mybir
from contextlib import ExitStack

F32 = mybir.dt.float32
I32 = mybir.dt.int32
U32 = mybir.dt.uint32
ALU = mybir.AluOpType
ACT = mybir.ActivationFunctionType
AX = mybir.AxisListType.X
RMAX = bass.bass_isa.ReduceOp.max
IND = bass.IndirectOffsetOnAxis
ds = bass.ds

P = 128
NODES, D = 6250, 256
EDGES = 200000
NT = -(-NODES // P)
NP = NT * P
KD = D // P
U = 8
NG = -(-EDGES // (P * U))
HEADS, HC = 8, 32
NH2 = 2 * HEADS
F = 1024
KF = F // P
E, TOPK = 8, 2
STEPS = NT * TOPK + E
PADROWS = NP + P
SLOTS = (E - 1) * NP + (STEPS - NT) * P
EPS = 1e-5
XCH = 7
RW = D + 2


class Own:

    def __init__(self, eng, sem, ready):
        self.eng, self.sem, self.ready = eng, sem, ready
        self.done = eng.alloc_register("own_done")
        eng.reg_mov(self.done, 0)

    def step(self, ins, constant_wait=False):
        ins.then_inc(self.sem, 1)
        self.eng.reg_add(self.done, self.done, 1)
        if constant_wait:
            self.eng.wait_ge(*self.ready)
        self.eng.wait_ge(self.sem, self.done)


def gps_layer(nc, x, idx, dst, wl, bl, wr, wln, wkv, bkv, wq, bq, kvg, kvb, w1, b1, w2, b2, wrt,
              w1s, b1s, w2s, b2s, w1p, b1p, w2p, b2p, ident, triu, valid, iota, tcol, eoff,
              hmask, slot0, out):
    ctx = ExitStack()
    with ctx:
        def sb(name, shape, dt=F32):
            return ctx.enter_context(nc.sbuf_tensor(name, shape, dt))

        def pb(name, shape):
            return ctx.enter_context(nc.psum_tensor(name, shape, F32))

        def sem(name):
            return ctx.enter_context(nc.semaphore(name))

        xn_d = nc.dram_tensor("xn_d", [NP, D], F32, kind="Internal").ap()
        xf_d = nc.dram_tensor("xf_d", [PADROWS, D], F32, kind="Internal").ap()
        slot_d = nc.dram_tensor("slot_d", [SLOTS, 2], I32, kind="Internal").ap()

        id_s = sb("id_s", [P, P])
        triu_s = sb("triu_s", [P, P])
        ones_s = sb("ones_s", [P, P])
        zero_s = sb("zero_s", [P, D])
        valid_s = sb("valid_s", [P, NT])
        iota_s = sb("iota_s", [P, P])
        tcol_s = sb("tcol_s", [P, NT + 1])
        eoff_s = sb("eoff_s", [P, E])
        wl_s = sb("wl_s", [P, KD, D])
        wr_s = sb("wr_s", [P, KD, D])
        wln_s = sb("wln_s", [P, KD, D])
        bl_s = sb("bl_s", [P, KD])
        wkv_s = sb("wkv_s", [P, KD, 2 * D])
        tabf_s = sb("tabf_s", [1, 5, P])
        bkv_s = tabf_s[:, 0:4, :].rearrange("p a b -> p (a b)")
        bq_s = sb("bq_s", [P, KD])
        kvg_s = sb("kvg_s", [P, 2 * HC])
        kvb_s = sb("kvb_s", [P, 2 * HC])
        w1_s = sb("w1_s", [P, KD, D])
        b1_s = sb("b1_s", [P, KD])
        w2_s = sb("w2_s", [P, KD, D])
        b2_s = sb("b2_s", [P, D])
        wrt_s = sb("wrt_s", [P, KD, E])
        w1s_s = sb("w1s_s", [P, KD, F])
        b1s_s = sb("b1s_s", [P, KF])
        w2s_s = sb("w2s_s", [P, KF, D])
        b2s_s = sb("b2s_s", [P, D])
        rows4 = sb("rows4", [P, 4, D])
        xr_s, x2_s, xf_s, o_s = (rows4[:, i, :] for i in range(4))
        hmask_s, wq_s = rows4[:, 0:2, :], rows4[:, 2:4, :]
        kv_s = sb("kv_s", [P, KD, D])
        m1_s = sb("m1_s", [P, KD, D])
        c1_s = sb("c1_s", [P, KD])

        region = sb("region", [P, E * KF * D])
        x_s = region[:, 0:NT * D].rearrange("p (t d) -> p t d", d=D)
        w2p_s = region[:, :].rearrange("p (e j d) -> p e j d", e=E, d=D)
        late = sb("late", [P, NT * RW])
        agg_s = late[:, :].rearrange("p (t d) -> p t d", d=RW)

        dst_s = sb("dst_s", [P, NG * U], I32)
        idx_s = [sb(f"idx_s{h}", [P, U], I32) for h in range(2)]
        ring = [sb(f"ring{h}", [P, U, RW]) for h in range(2)]
        onehot = sb("onehot", [P, U, P])
        tile_i = sb("tile_i", [1, 2 * NG], I32)
        ext_s = onehot[:, 0:4, :].rearrange("p a b -> p (a b)")[:, 0:2 * NG]
        extr_s = onehot[:, 4:8, :].rearrange("p a b -> p (a b)")[:, 0:2 * NG]
        span_s = sb("span_s", [1, 2 * NG], I32)

        w1p_s = [late[:, h * KD * F:(h + 1) * KD * F].rearrange("p (k f) -> p k f", f=F) for h in range(2)]
        b2p_s, xg_s, yg_s = ([late[:, 2 * KD * F + (2 * i + h) * D:][:, 0:D] for h in range(2)] for i in range(3))
        slot_s = [sb(f"slot_s{h}", [P, 2], I32) for h in range(2)]
        b1p_s = [sb(f"b1p_s{h}", [P, KF]) for h in range(2)]
        work = sb("work", [P, 4, 2 * D])
        cen_s, sq_s, kvn_s, kvh_s = (work[:, i, :] for i in range(4))
        hid_s = work[:, 0:2, :].rearrange("p a (b c) -> p (a b) c", c=P)
        t1_s, t2_s, t3_s, t4_s = (work[:, 2 + i // 2, i % 2 * D:(i % 2 + 1) * D] for i in range(4))
        xt_s = sb("xt_s", [P, 4, P])
        xft_s = sb("xft_s", [P, KD, P])
        act_s = sb("act_s", [P, 4, P])

        xnr_s = sb("xnr_s", [P, D])
        mean_s = sb("mean_s", [P, D])
        st_s = sb("st_s", [P, XCH, 6])
        mv_s = sb("mv_s", [P, XCH, 2])
        ve_s = sb("ve_s", [P, NH2])
        sd_s = sb("sd_s", [P, NH2])
        rs_s = sb("rs_s", [P, NH2])
        hm_s = sb("hm_s", [P, NH2])
        c_s = sb("c_s", [P, 2])
        rt_s = sb("rt_s", [P, 8, E])
        ri_s = sb("ri_s", [P, E], U32)
        oh_s = sb("oh_s", [P, TOPK, E])
        ohp_s = sb("ohp_s", [P, TOPK, E])
        sel_s = sb("sel_s", [P, E])
        base_s = sb("base_s", [P, E])
        rv_s = sb("rv_s", [P, 16])
        posi_s = sb("posi_s", [P, TOPK], I32)
        pay_s = sb("pay_s", [P, TOPK, 2], I32)
        tabi_s = sb("tabi_s", [1, 2, P], I32)
        nti_s = sb("nti_s", [1, 2, E], I32)
        ntf_s = sb("ntf_s", [1, 4, E])

        p_agg = pb("p_agg", [P, 512])
        p_t = pb("p_t", [P, 4, P])
        p_a = pb("p_a", [P, 4, P])
        p_b = pb("p_b", [P, 2, D])
        p_c = pb("p_c", [P, 2, D])
        p_h = [pb(f"p_h{i}", [P, 4, P]) for i in range(2)]
        p_y = pb("p_y", [P, 2, D])
        p_kv = p_a[:, :, :].rearrange("p a b -> p (a b)")

        names = """wts const xin xn xnst aggz ext extr span own_dve
            idx0 idx1 oneh pass_ added used0 used1
            kvx kvt kvtc proj cen sq ssq ve sd rsr kvh kvs kvm at atc bqk bqc m1p m1 c1p c1
            xr xnr mean tm tc sage mix1 relu g1 gnn mix2 x2 ve2 sd2 xf xfst txf xfc lg h gl y o ost
            mx ex sel cnt pay sc tab w2p
            slot0 slot1 w1p0 w1p1 xg0 xg1 yt ytc yh ygl yy yg0 yg1 scat""".split()
        S = {n: sem(f"s_{n}") for n in names}
        s_row = [[sem(f"s_row{h}_{u}") for u in range(U)] for h in range(2)]
        block = ctx.enter_context(nc.Block())

        def rows(ap, t, n=P):
            return ap[ds(t * n, n), :]

        loads = [(id_s[:, :], ident), (triu_s[:, :], triu), (valid_s[:, :], valid), (iota_s[:, :], iota),
                 (tcol_s[:, :], tcol), (eoff_s[:, :], eoff), (dst_s[:, :], dst), (wl_s[:, :, :], wl),
                 (wr_s[:, :, :], wr), (wln_s[:, :, :], wln), (bl_s[:, :], bl), (wkv_s[:, :, :], wkv),
                 (bkv_s[:, :], bkv), (wq_s[:, :, :], wq), (bq_s[:, :], bq), (kvg_s[:, :], kvg),
                 (kvb_s[:, :], kvb), (w1_s[:, :, :], w1), (b1_s[:, :], b1), (w2_s[:, :, :], w2),
                 (b2_s[:, :], b2), (wrt_s[:, :, :], wrt), (w1s_s[:, :, :], w1s), (b1s_s[:, :], b1s),
                 (w2s_s[:, :, :], w2s), (b2s_s[:, :], b2s), (hmask_s[:, :, :], hmask)]
        WTS = 16 * len(loads)

        @block.sync
        def _(sp):
            for c in range(NT // XCH):
                if c:
                    sp.wait_ge(S["xin"], 16 * c)
                sp.dma_start(x_s[:, c * XCH:(c + 1) * XCH, :],
                             x[c * XCH * P:(c + 1) * XCH * P, :].rearrange("(t p) d -> p t d", p=P)
                             ).then_inc(S["xin"], 16)
                if c == 0:
                    for to, of in loads:
                        sp.dma_start(to, of).then_inc(S["wts"], 16)
            sp.wait_ge(S["const"], 3)
            sp.dma_start(xf_d[NP:PADROWS, :], zero_s[:, :]).then_inc(S["xfst"], 16)
            sp.dma_start(out[NP:NP + P // 2, :], zero_s[0:P // 2, :]).then_inc(S["ost"], 16)
            sp.wait_ge(S["xnst"], 16 * (NT // XCH))
            sp.dma_start(w2p_s, w2p.rearrange("e (j p) d -> p e j d", p=P)).then_inc(S["w2p"], 16)

            def load_idx(it):
                for h in range(2):
                    sp.wait_ge(S[f"used{h}"], it + 1)
                    sp.dma_start(idx_s[h][:, :], idx[ds(2 * it + h, 1), :, :].squeeze(0)
                                 ).then_inc(S[f"idx{h}"], 16)

            with sp.Fori(0, NT) as it:
                sp.wait_ge(S["kvt"], it + 1)
                sp.dma_start(xnr_s[:, :], rows(xn_d, it)).then_inc(S["kvx"], 16)
                load_idx(it)
            with sp.Fori(NT, NG // 2) as it:
                load_idx(it)
            with sp.Fori(0, NT) as p:
                sp.wait_ge(S["x2"], p + 1)
                sp.dma_start(xr_s[:, :], rows(x, p)).then_inc(S["xr"], 16)
                sp.dma_start(xnr_s[:, :], rows(xn_d, p)).then_inc(S["xnr"], 16)
                sp.wait_ge(S["xf"], p + 1)
                sp.dma_start(rows(xf_d, p), xf_s[:, :]).then_inc(S["xfst"], 16)
                sp.wait_ge(S["o"], p + 2)
                sp.dma_start(rows(out, p), o_s[:, :]).then_inc(S["ost"], 16)
            sp.wait_ge(S["tab"], 1)
            sp.wait_ge(S["sc"], 16 * (2 * NT + 1))
            with sp.Fori(0, STEPS // 2) as it:
                for h in range(2):
                    s = 2 * it + h
                    e = sp.value_load(tabi_s[0:1, 0, ds(s, 1)], min_val=0, max_val=E - 1)
                    o = sp.value_load(tabi_s[0:1, 1, ds(s, 1)], min_val=0, max_val=SLOTS - P)
                    sp.wait_ge(S["scat"], 16 * s + 16)
                    sp.dma_start(slot_s[h][:, :], slot_d[ds(o, P), :]).then_inc(S[f"slot{h}"], 16)
                    sp.dma_start(w1p_s[h][:, :, :], w1p[ds(e, 1), :, :].squeeze(0).rearrange("(k p) f -> p k f", p=P)
                                 ).then_inc(S[f"w1p{h}"], 16)
                    sp.dma_start(b1p_s[h][:, :], b1p[ds(e, 1), :, :].squeeze(0)).then_inc(S[f"w1p{h}"], 16)
                    sp.dma_start(b2p_s[h][:, :], b2p[ds(e, 1), :].to_broadcast([P, D])).then_inc(S[f"w1p{h}"], 16)

        @block.gpsimd
        def _(pool):
            nc.gpsimd.memset(ones_s[:, :], 1.0).then_inc(S["const"], 1)
            nc.gpsimd.memset(zero_s[:, :], 0.0).then_inc(S["const"], 1)
            nc.gpsimd.memset(ring[0][:, :, D:RW], 1.0)
            nc.gpsimd.memset(ring[1][:, :, D:RW], 1.0).then_inc(S["const"], 1)
            pool.dma_start(slot_d.rearrange("(p c) w -> p (c w)", p=P), slot0.rearrange("(p c) w -> p (c w)", p=P)
                           ).then_inc(S["sc"], 16)
            pool.wait_ge(S["const"], 3)
            for i in (2, 3):
                pool.dma_start(out[NP + i * P // 4:NP + (i + 1) * P // 4, :], zero_s[0:P // 4, :]
                               ).then_inc(S["scat"], 16)
            pool.wait_ge(S["ext"], 1)
            nc.gpsimd.partition_all_reduce(extr_s[:, :], ext_s[:, :], P, RMAX).then_inc(S["extr"], 1)
            pool.wait_ge(S["xnst"], 16 * (NT // XCH))
            turn = pool.alloc_register("turn")
            turn16 = pool.alloc_register("turn16")
            pool.reg_mov(turn, 1)
            pool.reg_mov(turn16, 16)
            with pool.Fori(0, NG // 2) as it:
                for h in range(2):
                    pool.wait_ge(S["const"], 3)
                    pool.wait_ge(S[f"idx{h}"], turn16)
                    pool.wait_ge(S[f"used{h}"], turn)
                    for u in range(U):
                        pool.indirect_dma_start(
                            out=ring[h][:, u, 0:D], out_offset=None, in_=xn_d,
                            in_offset=IND(ap=idx_s[h][:, u:u + 1], axis=0)).then_inc(s_row[h][u], 16)
                pool.reg_add(turn, turn, 1)
                pool.reg_add(turn16, turn16, 16)
            pool.wait_ge(S["sc"], 16)
            pool.reg_mov(turn, 1)
            with pool.Fori(0, NT) as p:
                pool.wait_ge(S["const"], 3)
                pool.wait_ge(S["pay"], turn)
                for k in range(TOPK):
                    pool.indirect_dma_start(out=slot_d, out_offset=IND(ap=posi_s[:, k:k + 1], axis=0),
                                            in_=pay_s[:, k, :], in_offset=None).then_inc(S["sc"], 16)
                pool.reg_add(turn, turn, 1)
            pool.wait_ge(S["xfst"], 16 * NT + 16)
            pool.wait_ge(S["ost"], 16 * NT + 16)
            pool.reg_mov(turn, 1)
            pool.reg_mov(turn16, 16)
            turn2 = pool.alloc_register("turn2")
            pool.reg_mov(turn2, 2)
            done16 = pool.alloc_register("done16")
            pool.reg_mov(done16, 32)
            with pool.Fori(0, STEPS // 2) as it:
                for h in range(2):
                    pool.wait_ge(S["const"], 3)
                    pool.wait_ge(S[f"slot{h}"], turn16)
                    pool.indirect_dma_start(out=xg_s[h][:, :], out_offset=None, in_=xf_d,
                                            in_offset=IND(ap=slot_s[h][:, 0:1], axis=0)).then_inc(S[f"xg{h}"], 16)
                    pool.wait_ge(S["const"], 3)
                    pool.wait_ge(S[f"yg{h}"], turn if h == 0 else turn2)
                    pool.wait_ge(S["scat"], done16)
                    pool.indirect_dma_start(out=out, out_offset=IND(ap=slot_s[h][:, 0:1], axis=0),
                                            in_=yg_s[h][:, :], in_offset=None, compute_op=ALU.add
                                            ).then_inc(S["scat"], 16)
                    pool.reg_add(done16, done16, 16)
                pool.reg_add(turn, turn, 1)
                pool.reg_add(turn2, turn2, 1)
                pool.reg_add(turn16, turn16, 16)
            pool.wait_ge(S["scat"], 16 * STEPS + 32)

        @block.scalar
        def _(act):
            for n in ("kvtc", "sq"):
                act.sem_inc(S[n], 1)
            with act.Fori(0, NT // XCH) as c:
                act.wait_ge(S["ve"], c + 1)
                nc.scalar.activation(sd_s[:, 0:XCH], ve_s[:, 0:XCH], ACT.Sqrt).then_inc(S["sd"], 1)
                act.wait_ge(S["xn"], c + 1)
                act.dma_start(xn_d[ds(c * (XCH * P), XCH * P), :].rearrange("(t p) d -> p t d", p=P),
                              x_s[:, ds(c * XCH, XCH), :]).then_inc(S["xnst"], 16)
            with act.Fori(0, NT) as it:
                act.wait_ge(S["kvt"], it + 2)
                act.wait_ge(S["proj"], it + 1)
                nc.scalar.activation(xt_s[:, 0:2, :], p_t[:, 0:2, :], ACT.Copy).then_inc(S["kvtc"], 1)
                act.wait_ge(S["cen"], it + 2)
                nc.scalar.activation(sq_s[:, :], cen_s[:, :], ACT.Square).then_inc(S["sq"], 1)
                act.wait_ge(S["ve"], NT // XCH + 1 + it)
                nc.scalar.activation(sd_s[:, :], ve_s[:, :], ACT.Sqrt).then_inc(S["sd"], 1)
            act.wait_ge(S["bqk"], 1)
            nc.scalar.activation(c_s[:, 0:2], p_h[1][:, 0, 0:2], ACT.Copy).then_inc(S["bqc"], 1)
            for n in ("tc", "relu", "g1", "xfc", "gl", "ex"):
                act.sem_inc(S[n], 1)
            with act.Fori(0, NT) as p:
                act.wait_ge(S["tm"], p + 1)
                act.wait_ge(S["mix1"], p + 1)
                nc.scalar.activation(xt_s[:, :, :], p_t[:, :, :], ACT.Copy).then_inc(S["tc"], 1)
                act.wait_ge(S["sage"], p + 2)
                act.wait_ge(S["mix2"], p + 1)
                for j in range(KD):
                    r = nc.scalar.activation(act_s[:, j, :], p_a[:, j, :], ACT.Relu, bias=bl_s[:, j:j + 1])
                r.then_inc(S["relu"], 1)
                act.wait_ge(S["mix1"], p + 2)
                for j in range(KD):
                    r = nc.scalar.activation(act_s[:, 2 + j, :], p_h[0][:, j, :], ACT.Gelu, bias=c1_s[:, j:j + 1])
                r.then_inc(S["g1"], 1)
                act.wait_ge(S["ve2"], p + 1)
                nc.scalar.activation(sd_s[:, 0:1], ve_s[:, 0:1], ACT.Sqrt).then_inc(S["sd2"], 1)
                act.wait_ge(S["txf"], p + 1)
                act.wait_ge(S["cnt"], p + 1)
                nc.scalar.activation(xft_s[:, :, :], p_t[:, 0:KD, :], ACT.Copy).then_inc(S["xfc"], 1)
                act.wait_ge(S["mx"], p + 1)
                nc.scalar.activation(rt_s[:, 0, :], p_c[:, 0, 0:E], ACT.Exp, bias=rv_s[:, 1:2],
                                     accum_out=rv_s[:, 2:3]).then_inc(S["ex"], 1)
                act.wait_ge(S["y"], p + 1)
                for j in range(KF):
                    act.wait_ge(S["h"], p * KF + j + 1)
                    nc.scalar.activation(hid_s[:, j, :], p_h[j % 2][:, 0, :], ACT.Gelu,
                                         bias=b1s_s[:, j:j + 1]).then_inc(S["gl"], 1)
            act.sem_inc(S["ytc"], 1)
            act.sem_inc(S["ygl"], 1)
            with act.Fori(0, STEPS // 2) as it:
                for h in range(2):
                    s = 2 * it + h
                    act.wait_ge(S["yt"], s + 1)
                    act.wait_ge(S["yh"], s * KF + 1)
                    nc.scalar.activation(xft_s[:, :, :], p_t[:, 0:KD, :], ACT.Copy).then_inc(S["ytc"], 1)
                    act.wait_ge(S["yy"], s + 1)
                    act.wait_ge(S[f"w1p{h}"], 48 * (it + 1))
                    for j in range(KF):
                        act.wait_ge(S["yh"], s * KF + j + 2)
                        nc.scalar.activation(hid_s[:, j, :], p_h[j % 2][:, 0, :], ACT.Gelu,
                                             bias=b1p_s[h][:, j:j + 1]).then_inc(S["ygl"], 1)

        @block.vector
        def _(dve):
            V = nc.vector
            own = Own(dve, S["own_dve"], (S["const"], 3))
            for n in ("cen", "ssq", "x2", "o", "yg1"):
                dve.sem_inc(S[n], 1)
            V.memset(agg_s[:, :, :], 0.0)
            with dve.Fori(0, NT // XCH) as c:
                dve.wait_ge(S["xin"], 16 * c + 16)
                for j in range(XCH):
                    i = V.bn_stats(st_s[:, j, :], x_s[:, ds(c * XCH + j, 1), :])
                own.step(i, True)
                for j in range(XCH):
                    i = V.bn_aggr(mv_s[:, j, :], st_s[:, j, :])
                own.step(i)
                V.tensor_scalar(ve_s[:, 0:XCH], mv_s[:, :, 1:2].squeeze(2), EPS, None, ALU.add).then_inc(S["ve"], 1)
                dve.wait_ge(S["sd"], c + 1)
                own.step(V.reciprocal(rs_s[:, 0:XCH], sd_s[:, 0:XCH]))
                for j in range(XCH):
                    xj = x_s[:, ds(c * XCH + j, 1), :]
                    i = V.tensor_scalar(xj, xj, mv_s[:, j, 0:1], rs_s[:, j:j + 1], ALU.subtract, ALU.mult)
                i.then_inc(S["xn"], 1)
            dve.wait_ge(S["wts"], WTS)
            own.step(V.tensor_reduce(ext_s[:, 0:NG], dst_s[:, :].rearrange("p (g u) -> p g u", u=U), AX, ALU.max))
            own.step(V.tensor_reduce(ext_s[:, NG:], dst_s[:, :].rearrange("p (g u) -> p g u", u=U), AX, ALU.min))
            V.tensor_scalar(ext_s[:, NG:], ext_s[:, NG:], -1.0, None, ALU.mult).then_inc(S["ext"], 1)
            dve.wait_ge(S["extr"], 1)
            own.step(V.tensor_copy(tile_i[0:1, 0:NG], extr_s[0:1, 0:NG]))
            own.step(V.tensor_scalar(tile_i[0:1, NG:], extr_s[0:1, NG:], -1.0, None, ALU.mult))
            own.step(V.tensor_scalar(tile_i[0:1, :], tile_i[0:1, :], 7, None, ALU.arith_shift_right))
            own.step(V.tensor_scalar(span_s[0:1, 0:NG], tile_i[0:1, 0:NG], 1, None, ALU.add))
            V.tensor_copy(span_s[0:1, NG:], tile_i[0:1, NG:]).then_inc(S["span"], 1)
            q = dve.alloc_register("passes_dve")
            dve.reg_mov(q, 1)
            dve.sem_inc(S["added"], 1)
            dve.wait_ge(S["span"], 1)

            def aggregate(it, h):
                g = 2 * it + h
                hi = dve.value_load(span_s[0:1, ds(g, 1)], min_val=1, max_val=NT)
                lo = dve.value_load(span_s[0:1, ds(g + NG, 1)], min_val=0, max_val=NT - 1)
                with dve.Fori(lo, hi) as t:
                    t = dve.snap(t, min_val=0, max_val=NT - 1)
                    dve.wait_ge(S["pass_"], q)
                    V.scalar_tensor_tensor(
                        out=onehot[:, :, :], in0=dst_s[:, ds(g * U, U)].unsqueeze(2).to_broadcast([P, U, P]),
                        scalar=tcol_s[:, ds(t, 1)], in1=iota_s[:, :].unsqueeze(1).to_broadcast([P, U, P]),
                        op0=ALU.subtract, op1=ALU.is_equal).then_inc(S["oneh"], 1)
                    dve.wait_ge(S["added"], q)
                    dve.reg_add(q, q, 1)
                    dve.wait_ge(S["pass_"], q)
                    a = agg_s[:, ds(t, 1), :]
                    V.tensor_tensor(a, a, p_agg[:, 0:RW].unsqueeze(1), ALU.add).then_inc(S["added"], 1)

            with dve.Fori(0, NT) as it:
                aggregate(it, 0)
                dve.wait_ge(S["proj"], it + 2)
                kv3 = p_kv.rearrange("p (g c) -> p g c", c=HC)
                own.step(V.tensor_reduce(hm_s[:, :], kv3, AX, ALU.add))
                own.step(V.tensor_scalar(hm_s[:, :], hm_s[:, :], 1.0 / HC, None, ALU.mult))
                V.tensor_tensor(cen_s[:, :].rearrange("p (g c) -> p g c", c=HC), kv3,
                                hm_s[:, :].unsqueeze(2).to_broadcast([P, NH2, HC]), ALU.subtract).then_inc(S["cen"], 1)
                dve.wait_ge(S["sq"], it + 2)
                V.tensor_reduce(ve_s[:, :], sq_s[:, :].rearrange("p (g c) -> p g c", c=HC), AX, ALU.add
                                ).then_inc(S["ssq"], 1)
                dve.wait_ge(S["ssq"], it + 2)
                V.tensor_scalar(ve_s[:, :], ve_s[:, :], 1.0 / HC, EPS, ALU.mult, ALU.add).then_inc(S["ve"], 1)
                dve.wait_ge(S["sd"], NT // XCH + 1 + it)
                own.step(V.reciprocal(rs_s[:, :], sd_s[:, :]))
                own.step(V.tensor_scalar(rs_s[:, :], rs_s[:, :], valid_s[:, ds(it, 1)], None, ALU.mult))
                own.step(V.tensor_tensor(kvn_s[:, :].rearrange("p (g c) -> p g c", c=HC),
                                         cen_s[:, :].rearrange("p (g c) -> p g c", c=HC),
                                         rs_s[:, :].unsqueeze(2).to_broadcast([P, NH2, HC]), ALU.mult))
                for i in range(2):
                    part = kvn_s[:, i * D:(i + 1) * D].rearrange("p (g c) -> p g c", c=HC)
                    last = V.tensor_tensor(part, part, kvg_s[:, i * HC:(i + 1) * HC].unsqueeze(1).to_broadcast([P, HEADS, HC]), ALU.mult)
                own.step(last)
                dve.wait_ge(S["kvs"], it + 1)
                for i in range(2):
                    last = V.scalar_tensor_tensor(
                        out=kvh_s[:, i * D:(i + 1) * D].rearrange("p (g c) -> p g c", c=HC),
                        in0=kvb_s[:, i * HC:(i + 1) * HC].unsqueeze(1).to_broadcast([P, HEADS, HC]),
                        scalar=valid_s[:, ds(it, 1)],
                        in1=kvn_s[:, i * D:(i + 1) * D].rearrange("p (g c) -> p g c", c=HC),
                        op0=ALU.mult, op1=ALU.add)
                last.then_inc(S["kvh"], 1)
                aggregate(it, 1)
            dve.wait_ge(S["kvs"], NT + 2)
            own.step(V.tensor_copy(base_s[:, :], eoff_s[:, :]))
            for c, bank in enumerate((p_b, p_c)):
                last = V.scalar_tensor_tensor(out=kv_s[:, c, :], in0=bank[:, 0, :], scalar=1.0 / NODES,
                                              in1=hmask_s[:, c, :], op0=ALU.mult, op1=ALU.mult)
            last.then_inc(S["kvm"], 1)
            dve.wait_ge(S["at"], 1)
            for c, a in enumerate((mean_s, t1_s)):
                o = 1 - c
                last = V.tensor_copy(a[:, o * P:(o + 1) * P], p_y[:, c, o * P:(o + 1) * P])
                last = V.tensor_tensor(a[:, c * P:(c + 1) * P], p_y[:, c, c * P:(c + 1) * P], id_s[:, :], ALU.add)
            last.then_inc(S["atc"], 1)
            dve.wait_ge(S["m1"], 1)
            V.tensor_copy(m1_s[:, :, :], p_h[0][:, :, :].rearrange("p (c a) b -> p c (a b)", c=2))
            V.tensor_tensor(c1_s[:, :], p_h[1][:, 1, 0:2], b1_s[:, :], ALU.add).then_inc(S["c1"], 1)
            with dve.Fori(NT, NG // 2) as it:
                for h in range(2):
                    aggregate(it, h)

            with dve.Fori(0, NT) as p:
                own.step(V.tensor_scalar(c_s[:, 0:1], agg_s[:, ds(p, 1), D:D + 1].squeeze(1), 1.0, None, ALU.max))
                own.step(V.reciprocal(c_s[:, 1:2], c_s[:, 0:1]))
                V.tensor_scalar(mean_s[:, :], agg_s[:, ds(p, 1), 0:D].squeeze(1), c_s[:, 1:2], None, ALU.mult
                                ).then_inc(S["mean"], 1)
                dve.wait_ge(S["xr"], 16 * p + 16)
                dve.wait_ge(S["xnr"], 16 * p + 16)
                dve.wait_ge(S["gnn"], p + 2)
                own.step(V.tensor_tensor(t1_s[:, :], p_b[:, 0, :], xnr_s[:, :], ALU.add))
                own.step(V.scalar_tensor_tensor(out=t2_s[:, :], in0=t1_s[:, :], scalar=0.0, in1=xr_s[:, :],
                                                op0=ALU.max, op1=ALU.add))
                dve.wait_ge(S["mix2"], p + 2)
                own.step(V.tensor_tensor(t3_s[:, :], p_y[:, 0, :], xnr_s[:, :], ALU.add))
                own.step(V.tensor_tensor(t4_s[:, :], t3_s[:, :], b2_s[:, :], ALU.add))
                V.tensor_tensor(x2_s[:, :], t2_s[:, :], t4_s[:, :], ALU.add).then_inc(S["x2"], 1)
                dve.wait_ge(S["x2"], p + 2)
                own.step(V.bn_stats(st_s[:, 0, :], x2_s[:, :]), True)
                own.step(V.bn_aggr(mv_s[:, 0, :], st_s[:, 0, :]))
                V.tensor_scalar(ve_s[:, 0:1], mv_s[:, 0, 1:2], EPS, None, ALU.add).then_inc(S["ve2"], 1)
                dve.wait_ge(S["sd2"], p + 1)
                own.step(V.reciprocal(rs_s[:, 0:1], sd_s[:, 0:1]))
                dve.wait_ge(S["xfst"], 16 * p + 16)
                V.tensor_scalar(xf_s[:, :], x2_s[:, :], mv_s[:, 0, 0:1], rs_s[:, 0:1], ALU.subtract, ALU.mult
                                ).then_inc(S["xf"], 1)
                dve.wait_ge(S["lg"], p + 1)
                own.step(V.reduce_max(rv_s[:, 0:1], p_c[:, 0, 0:E], AX))
                V.tensor_scalar(rv_s[:, 1:2], rv_s[:, 0:1], -1.0, None, ALU.mult).then_inc(S["mx"], 1)
                dve.wait_ge(S["ex"], p + 2)
                own.step(V.reciprocal(rv_s[:, 3:4], rv_s[:, 2:3]))
                own.step(V.tensor_scalar(rt_s[:, 1, :], rt_s[:, 0, :], rv_s[:, 3:4], None, ALU.mult), True)
                own.step(V.max(rt_s[:, 2, :], rt_s[:, 1, :]), True)
                own.step(V.max_index(ri_s[:, :], rt_s[:, 2, :], rt_s[:, 1, :]))
                own.step(V.tensor_tensor(rv_s[:, 4:5], rt_s[:, 2, 0:1], rt_s[:, 2, 1:2], ALU.add))
                own.step(V.reciprocal(rv_s[:, 5:6], rv_s[:, 4:5]))
                own.step(V.tensor_copy(rv_s[:, 6:8], ri_s[:, 0:2]))
                own.step(V.tensor_tensor(oh_s[:, :, :], iota_s[:, 0:E].unsqueeze(1).to_broadcast([P, TOPK, E]),
                                         rv_s[:, 6:8].unsqueeze(2).to_broadcast([P, TOPK, E]), ALU.is_equal))
                V.tensor_tensor(sel_s[:, :], oh_s[:, 0, :], oh_s[:, 1, :], ALU.add).then_inc(S["sel"], 1)
                dve.wait_ge(S["cnt"], p + 2)
                own.step(V.tensor_tensor(rt_s[:, 3, :], p_c[:, 0, E:2 * E], base_s[:, :], ALU.add))
                V.tensor_tensor(base_s[:, :], p_c[:, 0, 2 * E:3 * E], base_s[:, :], ALU.add)
                own.step(V.tensor_tensor(ohp_s[:, :, :], oh_s[:, :, :],
                                         rt_s[:, 3, :].unsqueeze(1).to_broadcast([P, TOPK, E]), ALU.mult))
                own.step(V.tensor_reduce(rv_s[:, 8:10], ohp_s[:, :, :], AX, ALU.add))
                dve.wait_ge(S["sc"], 32 * p + 16)
                V.tensor_copy(posi_s[:, :], rv_s[:, 8:10])
                V.tensor_scalar(pay_s[:, :, 0], tcol_s[:, NT:NT + 1].to_broadcast([P, TOPK]),
                                tcol_s[:, ds(p, 1)], None, ALU.add)
                V.tensor_scalar(pay_s[:, :, 1].bitcast(F32), rt_s[:, 2, 0:2], rv_s[:, 5:6], None, ALU.mult
                                ).then_inc(S["pay"], 1)
                dve.wait_ge(S["y"], p + 2)
                dve.wait_ge(S["ost"], 16 * p + 16)
                own.step(V.tensor_tensor(t1_s[:, :], p_y[:, 0, :], x2_s[:, :], ALU.add))
                V.tensor_tensor(o_s[:, :], t1_s[:, :], b2s_s[:, :], ALU.add).then_inc(S["o"], 1)
            own.step(V.tensor_tensor(ntf_s[:, 0, :], base_s[0:1, :], eoff_s[0:1, :], ALU.subtract))
            own.step(V.tensor_scalar(nti_s[:, 0, :], ntf_s[:, 0, :], float(P - 1), None, ALU.add))
            own.step(V.tensor_scalar(nti_s[:, 1, :], nti_s[:, 0, :], 7, None, ALU.arith_shift_right))
            own.step(V.tensor_copy(ntf_s[:, 1, :], nti_s[:, 1, :]))
            own.step(V.memset(ntf_s[:, 2, :], 1.0))
            own.step(V.tensor_tensor_scan(out=ntf_s[:, 3, :], data0=ntf_s[:, 2, :], data1=ntf_s[:, 1, :],
                                          initial=0.0, op0=ALU.mult, op1=ALU.add))
            own.step(V.memset(tabf_s[:, :, :], 0.0))
            step_no = iota_s[0:1, 0:P]
            for e in range(E - 1):
                end = ntf_s[:, 3, e:e + 1]
                own.step(V.tensor_scalar(tabf_s[:, 2, :], step_no, end, ntf_s[:, 1, e:e + 1], ALU.is_ge, ALU.mult))
                own.step(V.tensor_tensor(tabf_s[:, 1, :], tabf_s[:, 1, :], tabf_s[:, 2, :], ALU.add))
                own.step(V.scalar_tensor_tensor(out=tabf_s[:, 3, :], in0=step_no, scalar=end,
                                                in1=tabf_s[:, 0, :], op0=ALU.is_ge, op1=ALU.add))
                own.step(V.tensor_copy(tabf_s[:, 0, :], tabf_s[:, 3, :]))
            own.step(V.tensor_tensor(tabf_s[:, 2, :], step_no, tabf_s[:, 1, :], ALU.subtract))
            own.step(V.tensor_scalar(tabf_s[:, 2, :], tabf_s[:, 2, :], float(P), None, ALU.mult))
            own.step(V.tensor_copy(tabi_s[:, 0, :], tabf_s[:, 0, :]))
            V.scalar_tensor_tensor(out=tabi_s[:, 1, :], in0=tabf_s[:, 0, :], scalar=float(NP),
                                   in1=tabf_s[:, 2, :], op0=ALU.mult, op1=ALU.add).then_inc(S["tab"], 1)
            with dve.Fori(0, STEPS // 2) as it:
                for h in range(2):
                    s = 2 * it + h
                    gate = slot_s[h][:, 1:2].bitcast(F32)
                    dve.wait_ge(S[f"w1p{h}"], 48 * it + 48)
                    dve.wait_ge(S[f"slot{h}"], 16 * it + 16)
                    own.step(V.tensor_scalar((t1_s, t2_s)[h][:, :], b2p_s[h][:, :], gate, None, ALU.mult))
                    dve.wait_ge(S["yy"], s + 2)
                    dve.wait_ge(S["scat"], 16 * s + 16)
                    V.scalar_tensor_tensor(out=yg_s[h][:, :], in0=p_y[:, 0, :], scalar=gate, in1=(t1_s, t2_s)[h][:, :],
                                           op0=ALU.mult, op1=ALU.add).then_inc(S[f"yg{h}"], 1)

        @block.tensor
        def _(pe):
            mm = nc.tensor.matmul
            pe.wait_ge(S["wts"], WTS)
            pe.wait_ge(S["const"], 3)
            pe.wait_ge(S["span"], 1)
            for n in ("kvt", "proj", "kvs", "pass_", "used0", "used1"):
                pe.sem_inc(S[n], 1)
            q = pe.alloc_register("passes_pe")
            pe.reg_mov(q, 1)

            def aggregate(it, h):
                g = 2 * it + h
                hi = pe.value_load(span_s[0:1, ds(g, 1)], min_val=1, max_val=NT)
                lo = pe.value_load(span_s[0:1, ds(g + NG, 1)], min_val=0, max_val=NT - 1)
                with pe.Fori(lo, hi):
                    pe.wait_ge(S["oneh"], q)
                    pe.wait_ge(S["added"], q)
                    pe.reg_add(q, q, 1)
                    for u in range(U):
                        pe.wait_ge(s_row[h][u], 16 * it + 16)
                        m = mm(p_agg[:, 0:RW], onehot[:, u, :], ring[h][:, u, :], start=u == 0, stop=u == U - 1)
                    m.then_inc(S["pass_"], 1)
                mm(p_c[:, 1, 0:2], id_s[:, :], ring[h][:, 0, D:RW], start=False, stop=False,
                   skip_group_check=True).then_inc(S[f"used{h}"], 1)

            def transpose(to, of):
                return nc.tensor.transpose(to, of, id_s[:, :])

            for bank in (p_b, p_c):
                mm(bank[:, 0, :], zero_s[:, 0:P], zero_s[:, :], start=True, stop=False, skip_group_check=True)
            with pe.Fori(0, NT) as it:
                aggregate(it, 0)
                pe.wait_ge(S["kvx"], 16 * it + 16)
                pe.wait_ge(S["kvtc"], it + 1)
                for k in range(KD):
                    m = transpose(p_t[:, k, :], xnr_s[:, k * P:(k + 1) * P])
                m.then_inc(S["kvt"], 1)
                pe.wait_ge(S["kvtc"], it + 2)
                pe.wait_ge(S["cen"], it + 1)
                for k in range(KD):
                    mm(p_kv, xt_s[:, k, :], wkv_s[:, k, :], start=k == 0, stop=False)
                mm(p_kv, ones_s[0:1, :], bkv_s[:, :], start=False, stop=True).then_inc(S["proj"], 1)
                aggregate(it, 1)
                pe.wait_ge(S["kvh"], it + 1)
                for c, bank in enumerate((p_b, p_c)):
                    m = mm(bank[:, 0, :], kvh_s[:, c * P:(c + 1) * P], kvh_s[:, D:], start=False, stop=False,
                           skip_group_check=True)
                m.then_inc(S["kvs"], 1)
            for bank in (p_b, p_c):
                m = mm(bank[:, 0, :], zero_s[:, 0:P], zero_s[:, :], start=False, stop=True, skip_group_check=True)
            m.then_inc(S["kvs"], 1)
            pe.wait_ge(S["kvm"], 1)
            for c in range(KD):
                for k in range(KD):
                    m = mm(p_y[:, c, :], kv_s[:, k, c * P:(c + 1) * P], wq_s[:, k, :], start=k == 0, stop=k == KD - 1)
            m.then_inc(S["at"], 1)
            for c in range(KD):
                for k in range(KD):
                    m = mm(p_h[1][:, 0, c:c + 1], kv_s[:, k, c * P:(c + 1) * P], bq_s[:, k:k + 1],
                           start=k == 0, stop=k == KD - 1)
            m.then_inc(S["bqk"], 1)
            pe.wait_ge(S["atc"], 1)
            at = (mean_s, t1_s)
            for c in range(KD):
                for k in range(KD):
                    mm(p_h[0][:, 2 * c:2 * c + 2, :].rearrange("p a b -> p (a b)"), at[k][:, c * P:(c + 1) * P], w1_s[:, k, :],
                       start=k == 0, stop=k == KD - 1)
            pe.wait_ge(S["bqc"], 1)
            for c in range(KD):
                for k in range(KD):
                    m = mm(p_h[1][:, 1, c:c + 1], w1_s[:, k, c * P:(c + 1) * P], c_s[:, k:k + 1],
                           start=k == 0, stop=k == KD - 1)
            m.then_inc(S["m1"], 1)
            with pe.Fori(NT, NG // 2) as it:
                for h in range(2):
                    aggregate(it, h)

            for n in ("mix1", "gnn", "mix2", "sage", "cnt", "y"):
                pe.sem_inc(S[n], 1)
            pe.wait_ge(S["c1"], 1)
            with pe.Fori(0, NT) as p:
                pe.wait_ge(S["xnr"], 16 * p + 16)
                pe.wait_ge(S["mean"], p + 1)
                pe.wait_ge(S["xfc"], p + 1)
                for k in range(KD):
                    transpose(p_t[:, k, :], xnr_s[:, k * P:(k + 1) * P])
                for k in range(KD):
                    m = transpose(p_t[:, 2 + k, :], mean_s[:, k * P:(k + 1) * P])
                m.then_inc(S["tm"], 1)
                pe.wait_ge(S["tc"], p + 2)
                pe.wait_ge(S["relu"], p + 1)
                for j in range(KD):
                    for k in range(KD):
                        mm(p_a[:, j, :], wl_s[:, k, j * P:(j + 1) * P], xt_s[:, 2 + k, :], start=k == 0, stop=False)
                    for k in range(KD):
                        m = mm(p_a[:, j, :], wr_s[:, k, j * P:(j + 1) * P], xt_s[:, k, :], start=False, stop=k == KD - 1)
                m.then_inc(S["sage"], 1)
                pe.wait_ge(S["gl"], p * KF + 1)
                for j in range(KD):
                    for k in range(KD):
                        m = mm(p_h[0][:, j, :], m1_s[:, k, j * P:(j + 1) * P], xt_s[:, k, :],
                               start=k == 0, stop=k == KD - 1)
                m.then_inc(S["mix1"], 1)
                pe.wait_ge(S["relu"], p + 2)
                pe.wait_ge(S["x2"], p + 1)
                for j in range(KD):
                    m = mm(p_b[:, 0, :], act_s[:, j, :], wln_s[:, j, :], start=j == 0, stop=j == KD - 1)
                m.then_inc(S["gnn"], 1)
                pe.wait_ge(S["g1"], p + 2)
                pe.wait_ge(S["o"], p + 1)
                for j in range(KD):
                    m = mm(p_y[:, 0, :], act_s[:, 2 + j, :], w2_s[:, j, :], start=j == 0, stop=j == KD - 1)
                m.then_inc(S["mix2"], 1)
                pe.wait_ge(S["xf"], p + 1)
                for k in range(KD):
                    m = transpose(p_t[:, k, :], xf_s[:, k * P:(k + 1) * P])
                m.then_inc(S["txf"], 1)
                pe.wait_ge(S["xfc"], p + 2)
                for k in range(KD):
                    m = mm(p_c[:, 0, 0:E], xft_s[:, k, :], wrt_s[:, k, :], start=k == 0, stop=k == KD - 1)
                m.then_inc(S["lg"], 1)

                def up(j):
                    pe.wait_ge(S["gl"], p * KF + max(j - 1, 0) + 1)
                    for k in range(KD):
                        m = mm(p_h[j % 2][:, 0, :], w1s_s[:, k, j * P:(j + 1) * P], xft_s[:, k, :],
                               start=k == 0, stop=k == KD - 1)
                    m.then_inc(S["h"], 1)

                def down(j):
                    pe.wait_ge(S["gl"], p * KF + j + 2)
                    return mm(p_y[:, 0, :], hid_s[:, j, :], w2s_s[:, j, :], start=j == 0, stop=j == KF - 1)

                up(0)
                up(1)
                for j in range(KF):
                    m = down(j)
                    if j + 2 < KF:
                        up(j + 2)
                m.then_inc(S["y"], 1)
                pe.wait_ge(S["sel"], p + 1)
                mm(p_c[:, 0, E:2 * E], triu_s[:, :], sel_s[:, :], start=True, stop=True)
                mm(p_c[:, 0, 2 * E:3 * E], ones_s[:, :], sel_s[:, :], start=True, stop=True).then_inc(S["cnt"], 1)
            pe.sem_inc(S["yh"], 1)
            pe.sem_inc(S["yy"], 1)
            pe.wait_ge(S["w2p"], 16)
            pe.wait_ge(S["tab"], 1)
            with pe.Fori(0, STEPS // 2) as it:
                for h in range(2):
                    s = 2 * it + h
                    e = pe.value_load(tabi_s[0:1, 0, ds(s, 1)], min_val=0, max_val=E - 1)
                    pe.wait_ge(S[f"xg{h}"], 16 * it + 16)
                    pe.wait_ge(S["ytc"], s + 1)
                    for k in range(KD):
                        m = transpose(p_t[:, k, :], xg_s[h][:, k * P:(k + 1) * P])
                    m.then_inc(S["yt"], 1)
                    pe.wait_ge(S["ytc"], s + 2)
                    pe.wait_ge(S[f"w1p{h}"], 48 * it + 48)
                    pe.wait_ge(S[f"yg{1 - h}"], it + 1)

                    def up(j):
                        pe.wait_ge(S["ygl"], s * KF + max(j - 1, 0) + 1)
                        for k in range(KD):
                            m = mm(p_h[j % 2][:, 0, :], w1p_s[h][:, k, j * P:(j + 1) * P], xft_s[:, k, :],
                                   start=k == 0, stop=k == KD - 1)
                        m.then_inc(S["yh"], 1)

                    def down(j):
                        pe.wait_ge(S["ygl"], s * KF + j + 2)
                        return mm(p_y[:, 0, :], hid_s[:, j, :],
                                  w2p_s[:, ds(e, 1), j, :].squeeze(1), start=j == 0, stop=j == KF - 1)

                    up(0)
                    up(1)
                    for j in range(KF):
                        m = down(j)
                        if j + 2 < KF:
                            up(j + 2)
                    m.then_inc(S["yy"], 1)


_WEIGHTS = ["wl", "bl", "wr", "wln", "wkv", "bkv", "wq", "bq", "kvg", "kvb", "w1", "b1", "w2", "b2", "wrt",
            "w1s", "b1s", "w2s", "b2s", "w1p", "b1p", "w2p", "b2p"]
_CONSTS = ["ident", "triu", "valid", "iota", "tcol", "eoff", "hmask", "slot0"]


def kernel(**inputs):
    import numpy as np
    import concourse.bacc as bacc
    from concourse.bass_utils import run_bass_kernel_spmd as run

    v = {k: np.asarray(a) for k, a in inputs.items()}

    def by_rows(w):
        return w.reshape(w.shape[0] // P, P, -1).transpose(1, 0, 2)

    def column(b):
        return b.reshape(-1, P).T

    def wide(b):
        return np.broadcast_to(b.reshape(1, -1), (P, b.size))

    qkv = v["L0_mix_w_qkv"].reshape(D, HEADS, 3, HC)
    bqkv = v["L0_mix_b_qkv"].reshape(HEADS, 3, HC)
    x = np.zeros((NP, D), np.float32)
    x[:NODES] = v["x"]
    src = np.zeros(NG * U * P, np.int32)
    src[:EDGES] = v["src"]
    dst = np.full(NG * U * P, NP - 1, np.int32)
    dst[:EDGES] = v["dst"]
    slot0 = np.zeros((SLOTS, 2), np.int32)
    slot0[:, 0] = NP + np.arange(SLOTS) % P
    a = {
        "x": x,
        "idx": src.reshape(NG, U, P).transpose(0, 2, 1),
        "dst": dst.reshape(NG * U, P).T,
        "wl": by_rows(v["L0_gnn_W_l"].T), "bl": column(v["L0_gnn_b_l"]),
        "wr": by_rows(v["L0_gnn_W_r"].T), "wln": by_rows(v["L0_gnn_W_ln"].T),
        "wkv": by_rows(np.concatenate([qkv[:, :, 1].reshape(D, D), qkv[:, :, 2].reshape(D, D)], 1)),
        "bkv": np.concatenate([bqkv[:, 1].reshape(1, D), bqkv[:, 2].reshape(1, D)], 1),
        "wq": by_rows(qkv[:, :, 0].reshape(D, D).T), "bq": column(bqkv[:, 0].reshape(D)),
        "kvg": wide(np.concatenate([v["L0_mix_kln_g"], v["L0_mix_vln_g"]])),
        "kvb": wide(np.concatenate([v["L0_mix_kln_b"], v["L0_mix_vln_b"]])),
        "w1": by_rows(v["L0_mix_w1"]), "b1": column(v["L0_mix_b1"]),
        "w2": by_rows(v["L0_mix_w2"]), "b2": wide(v["L0_mix_b2"]),
        "wrt": by_rows(v["L0_ffn_Wr"]),
        "w1s": by_rows(v["L0_ffn_W1s"]), "b1s": column(v["L0_ffn_b1s"]),
        "w2s": by_rows(v["L0_ffn_W2s"]), "b2s": wide(v["L0_ffn_b2s"]),
        "w1p": v["L0_ffn_W1p"], "b1p": v["L0_ffn_b1p"].reshape(E, KF, P).transpose(0, 2, 1),
        "w2p": v["L0_ffn_W2p"], "b2p": v["L0_ffn_b2p"],
        "ident": np.eye(P, dtype=np.float32),
        "triu": np.triu(np.ones((P, P), np.float32), 1),
        "valid": (np.arange(NP).reshape(NT, P).T < NODES).astype(np.float32),
        "iota": np.broadcast_to(np.arange(P, dtype=np.float32), (P, P)),
        "tcol": np.concatenate([np.broadcast_to(P * np.arange(NT, dtype=np.float32), (P, NT)),
                                np.arange(P, dtype=np.float32)[:, None]], 1),
        "eoff": np.broadcast_to(NP * np.arange(E, dtype=np.float32), (P, E)),
        "hmask": by_rows(np.kron(np.eye(HEADS, dtype=np.float32), np.ones((HC, HC), np.float32))),
        "slot0": slot0,
    }
    nc = bacc.Bacc("TRN2", target_bir_lowering=False, num_devices=1)
    arrays, args = {}, {}
    for name in ["x", "idx", "dst"] + _WEIGHTS + _CONSTS:
        arr = np.ascontiguousarray(a[name])
        arrays[f"in_{name}"] = arr
        args[name] = nc.dram_tensor(f"in_{name}", arr.shape, mybir.dt.from_np(arr.dtype), kind="ExternalInput").ap()
    out = nc.dram_tensor("out_rows", (PADROWS, D), F32, kind="ExternalOutput").ap()
    gps_layer(nc, out=out, **args)
    r = run(nc, [arrays], core_ids=[0])
    return r.results[0]["out_rows"][:NODES]
```

```python
import concourse.bass as bass
from concourse import mybir
from contextlib import ExitStack

F32 = mybir.dt.float32
I32 = mybir.dt.int32
U32 = mybir.dt.uint32
ALU = mybir.AluOpType
ACT = mybir.ActivationFunctionType
AX = mybir.AxisListType.X
RMAX = bass.bass_isa.ReduceOp.max
IND = bass.IndirectOffsetOnAxis
ds = bass.ds

P = 128
NODES, D = 6250, 256
EDGES = 200000
NT = -(-NODES // P)
NP = NT * P
KD = D // P
NKV = NT + NT % 2
U = 4
RING = 4
NI = -(-EDGES // (P * U * RING))
NG = NI * RING
HEADS, HC = 8, 32
NH2 = 2 * HEADS
F = 1024
KF = F // P
E, TOPK = 8, 2
STEPS = NT * TOPK + E
AHEAD = 2
LISTED = 2 * AHEAD
PADROWS = NP + P
SLOTS = (E - 1) * NP + (STEPS + LISTED - NT) * P
EPS = 1e-5
XCH = 7
RW = D + 2


class Own:

    def __init__(self, eng, sem, ready):
        self.eng, self.sem, self.ready = eng, sem, ready
        self.done = eng.alloc_register("own_done")
        eng.reg_mov(self.done, 0)

    def step(self, ins, constant_wait=False):
        ins.then_inc(self.sem, 1)
        self.eng.reg_add(self.done, self.done, 1)
        if constant_wait:
            self.eng.wait_ge(*self.ready)
        self.eng.wait_ge(self.sem, self.done)


def gps_layer(nc, x, idx, dst, wl, bl, wr, wln, wkv, bkv, wq, bq, kvg, kvb, w1, b1, w2, b2, wrt,
              w1s, b1s, w2s, b2s, w1p, b1p, w2p, b2p, ident, triu, valid, iota, tcol, eoff,
              hmask, slot0, out):
    ctx = ExitStack()
    with ctx:
        def sb(name, shape, dt=F32):
            return ctx.enter_context(nc.sbuf_tensor(name, shape, dt))

        def pb(name, shape):
            return ctx.enter_context(nc.psum_tensor(name, shape, F32))

        def sem(name):
            return ctx.enter_context(nc.semaphore(name))

        xn_d = nc.dram_tensor("xn_d", [NKV * P, D], F32, kind="Internal").ap()
        xf_d = nc.dram_tensor("xf_d", [PADROWS, D], F32, kind="Internal").ap()
        slot_d = nc.dram_tensor("slot_d", [SLOTS, 2], I32, kind="Internal").ap()

        id_s = sb("id_s", [P, P])
        triu_s = sb("triu_s", [P, P])
        ones_s = sb("ones_s", [P, P])
        zero_s = sb("zero_s", [P, D])
        valid_s = sb("valid_s", [P, NKV])
        iota_s = sb("iota_s", [P, P])
        tcol_s = sb("tcol_s", [P, NT + 1])
        eoff_s = sb("eoff_s", [P, E])
        wl_s = sb("wl_s", [P, KD, D])
        wr_s = sb("wr_s", [P, KD, D])
        wln_s = sb("wln_s", [P, KD, D])
        bl_s = sb("bl_s", [P, KD])
        wkv_s = sb("wkv_s", [P, KD, 2 * D])
        tabf_s = sb("tabf_s", [1, 5, P])
        bkv_s = tabf_s[:, 0:4, :].rearrange("p a b -> p (a b)")
        bq_s = sb("bq_s", [P, KD])
        kvg_s = sb("kvg_s", [P, 2 * HC])
        kvb_s = sb("kvb_s", [P, 2 * HC])
        w1_s = sb("w1_s", [P, KD, D])
        b1_s = sb("b1_s", [P, KD])
        w2_s = sb("w2_s", [P, KD, D])
        b2_s = sb("b2_s", [P, D])
        wrt_s = sb("wrt_s", [P, KD, E])
        w1s_s = sb("w1s_s", [P, KD, F])
        b1s_s = sb("b1s_s", [P, KF])
        w2s_s = sb("w2s_s", [P, KF, D])
        b2s_s = sb("b2s_s", [P, D])
        rows4 = sb("rows4", [P, 4, D])
        xr_s, x2_s, xf_s, o_s = (rows4[:, i, :] for i in range(4))
        hmask_s, wq_s = rows4[:, 0:2, :], rows4[:, 2:4, :]
        kv_s = sb("kv_s", [P, KD, D])
        m1_s = sb("m1_s", [P, KD, D])
        c1_s = sb("c1_s", [P, KD])

        region = sb("region", [P, E * KF * D])
        x_s = region[:, 0:NT * D].rearrange("p (t d) -> p t d", d=D)
        w2p_s = region[:, :].rearrange("p (e j d) -> p e j d", e=E, d=D)
        late = sb("late", [P, NT * RW])
        agg_s = late[:, :].rearrange("p (t d) -> p t d", d=RW)

        dst_s = sb("dst_s", [P, (NG + 1) * U], I32)
        idx_s = [sb(f"idx_s{b}", [P, U], I32) for b in range(RING)]
        ring = [sb(f"ring{b}", [P, U, RW]) for b in range(RING)]
        onehot = sb("onehot", [P, 2, U, P])
        NS = NG + 1
        span_s = sb("span_s", [1, 2 * NS], I32)
        tile_i = onehot[0:1, :, :, :].rearrange("p a b c -> p (a b c)")[:, 0:2 * NS].bitcast(I32)

        w1p_s = [late[:, h * KD * F:(h + 1) * KD * F].rearrange("p (k f) -> p k f", f=F) for h in range(2)]
        after = 2 * KD * F
        xg_s, yg_s, gb2_s = ([late[:, after + (2 * i + h) * D:][:, 0:D] for h in range(2)] for i in range(3))
        after += 6 * D
        b2p_s = late[:, after:after + E * D].rearrange("p (e d) -> p e d", d=D)
        b1p_s = late[:, after + E * D:after + E * (D + KF)].rearrange("p (e j) -> p e j", j=KF)
        after += E * (D + KF)
        slots_s = late[:, after:after + 2 * (STEPS + LISTED)].bitcast(I32).rearrange("p (s w) -> p s w", w=2)
        tick_s = [late[0:1, after + 2 * (STEPS + LISTED) + h * KF:][:, 0:KF] for h in range(2)]
        gtok_s = [sb(f"gtok_s{h}", [P, 1], I32) for h in range(2)]
        stok_s = [sb(f"stok_s{h}", [P, 1], I32) for h in range(2)]
        gate_s = [sb(f"gate_s{h}", [P, 1]) for h in range(2)]
        b1_h = [sb(f"b1_h{h}", [P, KF]) for h in range(2)]
        work = sb("work", [P, 4, 2 * D])
        flat = work[:, :, :].rearrange("p a b -> p (a b)")
        ext_s, extr_s = flat[:, 0:2 * NS], flat[:, 2 * NS:4 * NS]
        cen_s, sq_s, kvn_s, kvh_s = (work[:, i, :] for i in range(4))
        hid_s = work[:, 0:2, :].rearrange("p a (b c) -> p (a b) c", c=P)
        t1_s, t2_s, t3_s, t4_s = (work[:, 2 + i // 2, i % 2 * D:(i % 2 + 1) * D] for i in range(4))
        xt_s = sb("xt_s", [P, 4, P])
        xft_s = sb("xft_s", [P, KD, P])
        yxt_s = (xft_s[:, :, :], xt_s[:, 0:KD, :])
        act_s = sb("act_s", [P, 4, P])

        xnr_s = sb("xnr_s", [P, D])
        mean_s = sb("mean_s", [P, D])
        st_s = sb("st_s", [P, XCH, 6])
        mv_s = sb("mv_s", [P, XCH, 2])
        ve_s = sb("ve_s", [P, NH2])
        sd_s = sb("sd_s", [P, NH2])
        rs_s = sb("rs_s", [P, NH2])
        hm_s = sb("hm_s", [P, NH2])
        c_s = sb("c_s", [P, 2])
        rt_s = sb("rt_s", [P, 8, E])
        ri_s = sb("ri_s", [P, E], U32)
        oh_s = sb("oh_s", [P, TOPK, E])
        ohp_s = sb("ohp_s", [P, TOPK, E])
        sel_s = sb("sel_s", [P, E])
        base_s = sb("base_s", [P, E])
        rv_s = sb("rv_s", [P, 16])
        posi_s = sb("posi_s", [P, TOPK], I32)
        pay_s = sb("pay_s", [P, TOPK, 2], I32)
        tabi_s = sb("tabi_s", [1, 3, P], I32)
        nti_s = sb("nti_s", [1, 2, E], I32)
        ntf_s = sb("ntf_s", [1, 4, E])

        p_agg0 = pb("p_agg0", [P, 512])
        p_t = pb("p_t", [P, 4, P])
        p_a = pb("p_a", [P, 4, P])
        p_agg1 = pb("p_agg1", [P, 512])
        p_c = pb("p_c", [P, 2, D])
        p_h = [pb(f"p_h{i}", [P, 4, P]) for i in range(2)]
        p_y = pb("p_y", [P, 2, D])
        p_kv = p_a[:, :, :].rearrange("p a b -> p (a b)")

        kvx_s = (xnr_s, mean_s)
        p_agg = (p_agg0[:, 0:RW], p_agg1[:, 0:RW])
        p_gnn = p_a[:, 2:4, :].rearrange("p a b -> p (a b)")
        y_bank = (p_y[:, 0, :], p_agg1[:, 0:D])
        _unused = ()

        names = """wts const xin xn xnst aggz ext extr span own_dve
            idx0 idx1 idx2 idx3 oneh pass_ added xoneh xpass
            kvx0 kvx1 kvt kvtc proj cen sq ssq ve sd rsr kvh kvs kvm at atc bqk bqc m1p m1 c1p c1
            xr xnr mean tm tc sage mix1 relu g1 gnn mix2 x2 ve2 sd2 xf xfst txf xfc lg h gl y o ost
            mx ex sel cnt pay sc tab w2p
            slots0 slots1 bp w1p0 w1p1 gtok0 gtok1 bias0 bias1 xg0 xg1 yt ytc yh ygl yy yg0 yg1 scat""".split()
        S = {n: sem(f"s_{n}") for n in names}
        s_row = [[sem(f"s_row{b}_{u}") for u in range(U)] for b in range(RING)]
        block = ctx.enter_context(nc.Block())

        def rows(ap, t, n=P):
            return ap[ds(t * n, n), :]

        loads = [(id_s[:, :], ident), (triu_s[:, :], triu), (valid_s[:, :], valid), (iota_s[:, :], iota),
                 (tcol_s[:, :], tcol), (eoff_s[:, :], eoff), (dst_s[:, :], dst), (wl_s[:, :, :], wl),
                 (wr_s[:, :, :], wr), (wln_s[:, :, :], wln), (bl_s[:, :], bl), (wkv_s[:, :, :], wkv),
                 (bkv_s[:, :], bkv), (wq_s[:, :, :], wq), (bq_s[:, :], bq), (kvg_s[:, :], kvg),
                 (kvb_s[:, :], kvb), (w1_s[:, :, :], w1), (b1_s[:, :], b1), (w2_s[:, :, :], w2),
                 (b2_s[:, :], b2), (wrt_s[:, :, :], wrt), (w1s_s[:, :, :], w1s), (b1s_s[:, :], b1s),
                 (w2s_s[:, :, :], w2s), (b2s_s[:, :], b2s), (hmask_s[:, :, :], hmask)]
        WTS = 16 * (len(loads) + 1)

        @block.sync
        def _(sp):
            for c in range(NT // XCH):
                if c:
                    sp.wait_ge(S["xin"], 16 * c)
                sp.dma_start(x_s[:, c * XCH:(c + 1) * XCH, :],
                             x[c * XCH * P:(c + 1) * XCH * P, :].rearrange("(t p) d -> p t d", p=P)
                             ).then_inc(S["xin"], 16)
                if c == 0:
                    for to, of in loads:
                        sp.dma_start(to, of).then_inc(S["wts"], 16)
            sp.wait_ge(S["const"], 3)
            sp.dma_start(xf_d[NP:PADROWS, :], zero_s[:, :]).then_inc(S["xfst"], 16)
            sp.dma_start(out[NP:NP + P // 2, :], zero_s[0:P // 2, :]).then_inc(S["ost"], 16)
            sp.dma_start(xn_d[NT * P:NKV * P, :], zero_s[:, :]).then_inc(S["wts"], 16)
            sp.wait_ge(S["xnst"], 16 * (NT // XCH))
            sp.dma_start(w2p_s, w2p.rearrange("e (j p) d -> p e j d", p=P)).then_inc(S["w2p"], 16)

            def load_idx(b, it):
                sp.dma_start(idx_s[b][:, :], idx[ds(RING * it + b, 1), :, :].squeeze(0)).then_inc(S[f"idx{b}"], 16)

            def next_idx(b, it):
                for u in range(U):
                    sp.wait_ge(s_row[b][u], 16 * it + 16)
                load_idx(b, it + 1)

            def load_kvx(h, it):
                sp.dma_start(kvx_s[h][:, :], rows(xn_d, 2 * it + h)).then_inc(S[f"kvx{h}"], 16)

            for b in range(RING):
                load_idx(b, 0)
            for h in range(2):
                load_kvx(h, 0)
            with sp.Fori(0, NKV // 2 - 1) as it:
                for b in range(RING):
                    next_idx(b, it)
                    if b % 2 == 0:
                        sp.wait_ge(S["kvt"], 2 * it + b // 2 + 2)
                        load_kvx(b // 2, it + 1)
            with sp.Fori(NKV // 2 - 1, NI) as it:
                for b in range(RING):
                    next_idx(b, it)
            with sp.Fori(0, NT) as p:
                sp.wait_ge(S["x2"], p + 1)
                sp.dma_start(xr_s[:, :], rows(x, p)).then_inc(S["xr"], 16)
                sp.dma_start(xnr_s[:, :], rows(xn_d, p)).then_inc(S["xnr"], 16)
                sp.wait_ge(S["xf"], p + 1)
                sp.dma_start(rows(xf_d, p), xf_s[:, :]).then_inc(S["xfst"], 16)
                sp.wait_ge(S["o"], p + 2)
                sp.dma_start(rows(out, p), o_s[:, :]).then_inc(S["ost"], 16)
            sp.wait_ge(S["tab"], 1)
            sp.wait_ge(S["sc"], 16 * (2 * NT + 1))
            sp.dma_start(b1p_s, b1p.rearrange("e p j -> p e j")).then_inc(S["bp"], 16)
            sp.dma_start(b2p_s, b2p.unsqueeze(0).to_broadcast([P, E, D])).then_inc(S["bp"], 16)

            flag = sp.alloc_register("flag")

            def load_w1p(h, s):
                e = sp.value_load(tabi_s[0:1, 0, ds(s, 1)], min_val=0, max_val=E - 1)
                sp.dma_start(w1p_s[h][:, :, :], w1p[ds(e, 1), :, :].squeeze(0).rearrange("(k p) f -> p k f", p=P)
                             ).then_inc(S[f"w1p{h}"], 16)

            def load_slots(h, s):
                o = sp.value_load(tabi_s[0:1, 1, ds(s, 1)], min_val=0, max_val=SLOTS - P)
                sp.dma_start(slots_s[:, ds(s, 1), :].squeeze(1), slot_d[ds(o, P), :]).then_inc(S[f"slots{h}"], 16)

            for h in range(2):
                load_slots(h, h)
            for h in range(2):
                load_w1p(h, h)
            for h in range(2):
                sp.wait_ge(S[f"slots{h}"], 16)
                load_slots(h, h + 2)
            with sp.Fori(0, STEPS // 2) as it:
                for h in range(2):
                    s = 2 * it + h
                    sp.wait_ge(S[f"slots{h}"], 16 * it + 32)
                    load_slots(h, s + LISTED)
                    same = sp.value_load(tabi_s[0:1, 2, ds(s + AHEAD, 1)], min_val=0, max_val=1)
                    sp.reg_mov(flag, same)
                    with sp.If_lt(flag, 1):
                        sp.wait_ge(S["yh"], s * KF + KF)
                        load_w1p(h, s + AHEAD)
                    with sp.Else():
                        sp.wait_ge(S["yh"], s * KF + KF)
                        sp.dma_start(tick_s[h], w1p[0, 0:1, 0:KF]).then_inc(S[f"w1p{h}"], 16)
            for h in range(2):
                sp.wait_ge(S[f"w1p{h}"], 16 * (STEPS // 2 + 1))
                sp.wait_ge(S[f"slots{h}"], 16 * (STEPS // 2 + 2))

        @block.gpsimd
        def _(pool):
            nc.gpsimd.memset(ones_s[:, :], 1.0).then_inc(S["const"], 1)
            nc.gpsimd.memset(zero_s[:, :], 0.0).then_inc(S["const"], 1)
            for b in range(RING):
                last = nc.gpsimd.memset(ring[b][:, :, D:RW], 1.0)
            last.then_inc(S["const"], 1)
            pool.dma_start(slot_d.rearrange("(p c) w -> p (c w)", p=P), slot0.rearrange("(p c) w -> p (c w)", p=P)
                           ).then_inc(S["sc"], 16)
            pool.wait_ge(S["const"], 3)
            for i in (2, 3):
                pool.dma_start(out[NP + i * P // 4:NP + (i + 1) * P // 4, :], zero_s[0:P // 4, :]
                               ).then_inc(S["scat"], 16)
            pool.wait_ge(S["ext"], 1)
            nc.gpsimd.partition_all_reduce(extr_s[:, :], ext_s[:, :], P, RMAX).then_inc(S["extr"], 1)
            pool.wait_ge(S["xnst"], 16 * (NT // XCH))
            turn = pool.alloc_register("turn")
            turn16 = pool.alloc_register("turn16")
            group = pool.alloc_register("group")
            pool.reg_mov(group, 1)
            pool.reg_mov(turn16, 16)
            with pool.Fori(0, NI) as it:
                for b in range(RING):
                    pool.wait_ge(S["const"], 3)
                    pool.wait_ge(S[f"idx{b}"], turn16)
                    pool.wait_ge(S["pass_"], group)
                    for u in range(U):
                        pool.indirect_dma_start(
                            out=ring[b][:, u, 0:D], out_offset=None, in_=xn_d,
                            in_offset=IND(ap=idx_s[b][:, u:u + 1], axis=0)).then_inc(s_row[b][u], 16)
                    pool.reg_add(group, group, 1)
                pool.reg_add(turn16, turn16, 16)
            pool.wait_ge(S["sc"], 16)
            pool.reg_mov(turn, 1)
            with pool.Fori(0, NT) as p:
                pool.wait_ge(S["const"], 3)
                pool.wait_ge(S["pay"], turn)
                for k in range(TOPK):
                    pool.indirect_dma_start(out=slot_d, out_offset=IND(ap=posi_s[:, k:k + 1], axis=0),
                                            in_=pay_s[:, k, :], in_offset=None).then_inc(S["sc"], 16)
                pool.reg_add(turn, turn, 1)
            pool.wait_ge(S["xfst"], 16 * NT + 16)
            pool.wait_ge(S["ost"], 16 * NT + 16)
            def gather(h):
                pool.indirect_dma_start(out=xg_s[h][:, :], out_offset=None, in_=xf_d,
                                        in_offset=IND(ap=gtok_s[h][:, 0:1], axis=0)).then_inc(S[f"xg{h}"], 16)

            for h in range(2):
                pool.wait_ge(S[f"gtok{h}"], 1)
                gather(h)
            turn2 = pool.alloc_register("turn2")
            pool.reg_mov(turn2, 2)
            tile1 = pool.alloc_register("tile1")
            pool.reg_mov(tile1, 1)
            done16 = pool.alloc_register("done16")
            pool.reg_mov(done16, 32)
            with pool.Fori(0, STEPS // 2) as it:
                for h in range(2):
                    pool.wait_ge(S["const"], 3)
                    pool.wait_ge(S[f"gtok{h}"], turn2)
                    pool.wait_ge(S["yt"], tile1)
                    gather(h)
                    pool.wait_ge(S["const"], 3)
                    pool.wait_ge(S[f"yg{h}"], turn2)
                    pool.wait_ge(S["scat"], done16)
                    pool.indirect_dma_start(out=out, out_offset=IND(ap=stok_s[h][:, 0:1], axis=0),
                                            in_=yg_s[h][:, :], in_offset=None, compute_op=ALU.add
                                            ).then_inc(S["scat"], 16)
                    pool.reg_add(done16, done16, 16)
                    pool.reg_add(tile1, tile1, 1)
                pool.reg_add(turn2, turn2, 1)
            pool.wait_ge(S["scat"], 16 * STEPS + 32)
            for h in range(2):
                pool.wait_ge(S[f"xg{h}"], 16 * (STEPS // 2 + 1))

        @block.scalar
        def _(act):
            for n in ("kvtc", "sq"):
                act.sem_inc(S[n], 1)
            with act.Fori(0, NT // XCH) as c:
                act.wait_ge(S["ve"], c + 1)
                nc.scalar.activation(sd_s[:, 0:XCH], ve_s[:, 0:XCH], ACT.Sqrt).then_inc(S["sd"], 1)
                act.wait_ge(S["xn"], c + 1)
                act.dma_start(xn_d[ds(c * (XCH * P), XCH * P), :].rearrange("(t p) d -> p t d", p=P),
                              x_s[:, ds(c * XCH, XCH), :]).then_inc(S["xnst"], 16)
            with act.Fori(0, NKV) as m:
                act.wait_ge(S["kvt"], m + 2)
                act.wait_ge(S["proj"], m + 1)
                nc.scalar.activation(xt_s[:, 0:2, :], p_t[:, 0:2, :], ACT.Copy).then_inc(S["kvtc"], 1)
                act.wait_ge(S["cen"], m + 2)
                nc.scalar.activation(sq_s[:, :], cen_s[:, :], ACT.Square).then_inc(S["sq"], 1)
                act.wait_ge(S["ve"], m + NT // XCH + 1)
                nc.scalar.activation(sd_s[:, :], ve_s[:, :], ACT.Sqrt).then_inc(S["sd"], 1)
            act.wait_ge(S["bqk"], 1)
            nc.scalar.activation(c_s[:, 0:2], p_h[1][:, 0, 0:2], ACT.Copy).then_inc(S["bqc"], 1)
            for n in ("tc", "relu", "g1", "xfc", "gl", "ex"):
                act.sem_inc(S[n], 1)
            with act.Fori(0, NT) as p:
                act.wait_ge(S["tm"], p + 1)
                act.wait_ge(S["mix1"], p + 1)
                nc.scalar.activation(xt_s[:, :, :], p_t[:, :, :], ACT.Copy).then_inc(S["tc"], 1)
                act.wait_ge(S["sage"], p + 2)
                act.wait_ge(S["mix2"], p + 1)
                for j in range(KD):
                    r = nc.scalar.activation(act_s[:, j, :], p_a[:, j, :], ACT.Relu, bias=bl_s[:, j:j + 1])
                r.then_inc(S["relu"], 1)
                act.wait_ge(S["mix1"], p + 2)
                for j in range(KD):
                    r = nc.scalar.activation(act_s[:, 2 + j, :], p_h[0][:, j, :], ACT.Gelu, bias=c1_s[:, j:j + 1])
                r.then_inc(S["g1"], 1)
                act.wait_ge(S["ve2"], p + 1)
                nc.scalar.activation(sd_s[:, 0:1], ve_s[:, 0:1], ACT.Sqrt).then_inc(S["sd2"], 1)
                act.wait_ge(S["txf"], p + 1)
                act.wait_ge(S["cnt"], p + 1)
                nc.scalar.activation(xft_s[:, :, :], p_t[:, 0:KD, :], ACT.Copy).then_inc(S["xfc"], 1)
                act.wait_ge(S["mx"], p + 1)
                nc.scalar.activation(rt_s[:, 0, :], p_c[:, 0, 0:E], ACT.Exp, bias=rv_s[:, 1:2],
                                     accum_out=rv_s[:, 2:3]).then_inc(S["ex"], 1)
                act.wait_ge(S["y"], p + 1)
                for j in range(KF):
                    act.wait_ge(S["h"], p * KF + j + 1)
                    nc.scalar.activation(hid_s[:, j, :], p_h[j % 2][:, 0, :], ACT.Gelu,
                                         bias=b1s_s[:, j:j + 1]).then_inc(S["gl"], 1)
            act.sem_inc(S["ygl"], 2)

            def copy_xt(s, h):
                act.wait_ge(S["yt"], s + 1)
                nc.scalar.activation(yxt_s[h], p_t[:, 0:KD, :], ACT.Copy).then_inc(S["ytc"], 1)

            copy_xt(0, 0)
            with act.Fori(0, STEPS // 2) as it:
                for h in range(2):
                    s = 2 * it + h
                    act.wait_ge(S[f"bias{h}"], it + 1)
                    for j in range(KF):
                        act.wait_ge(S["yh"], s * KF + j + 1)
                        nc.scalar.activation(hid_s[:, j, :], p_h[j % 2][:, 0, :], ACT.Gelu,
                                             bias=b1_h[h][:, j:j + 1]).then_inc(S["ygl"], 1)
                        if j == KF // 2:
                            copy_xt(s + 1, 1 - h)

        @block.vector
        def _(dve):
            V = nc.vector
            own = Own(dve, S["own_dve"], (S["const"], 3))
            for n in ("cen", "ssq", "x2", "o", "yg0", "yg1"):
                dve.sem_inc(S[n], 1)
            V.memset(agg_s[:, :, :], 0.0)
            with dve.Fori(0, NT // XCH) as c:
                dve.wait_ge(S["xin"], 16 * c + 16)
                for j in range(XCH):
                    i = V.bn_stats(st_s[:, j, :], x_s[:, ds(c * XCH + j, 1), :])
                own.step(i, True)
                for j in range(XCH):
                    i = V.bn_aggr(mv_s[:, j, :], st_s[:, j, :])
                own.step(i)
                V.tensor_scalar(ve_s[:, 0:XCH], mv_s[:, :, 1:2].squeeze(2), EPS, None, ALU.add).then_inc(S["ve"], 1)
                dve.wait_ge(S["sd"], c + 1)
                own.step(V.reciprocal(rs_s[:, 0:XCH], sd_s[:, 0:XCH]))
                for j in range(XCH):
                    xj = x_s[:, ds(c * XCH + j, 1), :]
                    i = V.tensor_scalar(xj, xj, mv_s[:, j, 0:1], rs_s[:, j:j + 1], ALU.subtract, ALU.mult)
                i.then_inc(S["xn"], 1)
            dve.wait_ge(S["wts"], WTS)
            own.step(V.tensor_reduce(ext_s[:, 0:NS], dst_s[:, :].rearrange("p (g u) -> p g u", u=U), AX, ALU.max))
            own.step(V.tensor_reduce(ext_s[:, NS:], dst_s[:, :].rearrange("p (g u) -> p g u", u=U), AX, ALU.min))
            V.tensor_scalar(ext_s[:, NS:], ext_s[:, NS:], -1.0, None, ALU.mult).then_inc(S["ext"], 1)
            dve.wait_ge(S["extr"], 1)
            own.step(V.tensor_copy(tile_i[0:1, 0:NS], extr_s[0:1, 0:NS]))
            own.step(V.tensor_scalar(tile_i[0:1, NS:], extr_s[0:1, NS:], -1.0, None, ALU.mult))
            V.tensor_scalar(span_s[0:1, :], tile_i[0:1, :], 7, None, ALU.arith_shift_right).then_inc(S["span"], 1)
            dve.sem_inc(S["added"], 1)
            xq = dve.alloc_register("extra_dve")
            dve.reg_mov(xq, 1)
            dve.wait_ge(S["span"], 1)

            def hot(g, b, t):
                return V.scalar_tensor_tensor(
                    out=onehot[:, b % 2, :, :], in0=dst_s[:, ds(g * U, U)].unsqueeze(2).to_broadcast([P, U, P]),
                    scalar=tcol_s[:, ds(t, 1)], in1=iota_s[:, :].unsqueeze(1).to_broadcast([P, U, P]),
                    op0=ALU.subtract, op1=ALU.is_equal)

            def add(b, t):
                a = agg_s[:, ds(t, 1), :]
                return V.tensor_tensor(a, a, p_agg[b % 2].unsqueeze(1), ALU.add)

            lo_r, hi_r = dve.alloc_register("lo_dve"), dve.alloc_register("hi_dve")

            def prepare(g, b):
                hi = dve.value_load(span_s[0:1, ds(g, 1)], min_val=0, max_val=NT - 1)
                lo = dve.value_load(span_s[0:1, ds(g + NS, 1)], min_val=0, max_val=NT - 1)
                dve.reg_mov(lo_r, lo)
                dve.reg_mov(hi_r, hi)
                with dve.If_lt(lo_r, hi_r):
                    with dve.Fori(lo, hi) as t:
                        t = dve.snap(t, min_val=0, max_val=NT - 1)
                        hot(g, b, t).then_inc(S["xoneh"], 1)
                        dve.wait_ge(S["const"], 3)
                        dve.wait_ge(S["xpass"], xq)
                        own.step(add(b, t))
                        dve.reg_add(xq, xq, 1)
                hot(g, b, hi).then_inc(S["oneh"], 1)

            def finish(g, b):
                hi = dve.value_load(span_s[0:1, ds(g, 1)], min_val=0, max_val=NT - 1)
                dve.wait_ge(S["const"], 3)
                dve.wait_ge(S["pass_"], g + RING + 1)
                dve.wait_ge(S["added"], g + 1)
                add(b, hi).then_inc(S["added"], 1)

            def center(m):
                dve.wait_ge(S["proj"], m + 2)
                kv3 = p_kv.rearrange("p (g c) -> p g c", c=HC)
                own.step(V.tensor_reduce(hm_s[:, :], kv3, AX, ALU.add))
                own.step(V.tensor_scalar(hm_s[:, :], hm_s[:, :], 1.0 / HC, None, ALU.mult))
                V.tensor_tensor(cen_s[:, :].rearrange("p (g c) -> p g c", c=HC), kv3,
                                hm_s[:, :].unsqueeze(2).to_broadcast([P, NH2, HC]), ALU.subtract).then_inc(S["cen"], 1)
                dve.wait_ge(S["sq"], m + 2)
                V.tensor_reduce(ve_s[:, :], sq_s[:, :].rearrange("p (g c) -> p g c", c=HC), AX, ALU.add
                                ).then_inc(S["ssq"], 1)
                dve.wait_ge(S["ssq"], m + 2)
                V.tensor_scalar(ve_s[:, :], ve_s[:, :], 1.0 / HC, EPS, ALU.mult, ALU.add).then_inc(S["ve"], 1)

            def scale(m):
                dve.wait_ge(S["sd"], m + NT // XCH + 1)
                own.step(V.reciprocal(rs_s[:, :], sd_s[:, :]))
                own.step(V.tensor_scalar(rs_s[:, :], rs_s[:, :], valid_s[:, ds(m, 1)], None, ALU.mult))
                own.step(V.tensor_tensor(kvn_s[:, :].rearrange("p (g c) -> p g c", c=HC),
                                         cen_s[:, :].rearrange("p (g c) -> p g c", c=HC),
                                         rs_s[:, :].unsqueeze(2).to_broadcast([P, NH2, HC]), ALU.mult))
                for i in range(2):
                    part = kvn_s[:, i * D:(i + 1) * D].rearrange("p (g c) -> p g c", c=HC)
                    last = V.tensor_tensor(part, part, kvg_s[:, i * HC:(i + 1) * HC].unsqueeze(1).to_broadcast([P, HEADS, HC]), ALU.mult)
                own.step(last)
                dve.wait_ge(S["kvs"], m + 1)
                for i in range(2):
                    last = V.scalar_tensor_tensor(
                        out=kvh_s[:, i * D:(i + 1) * D].rearrange("p (g c) -> p g c", c=HC),
                        in0=kvb_s[:, i * HC:(i + 1) * HC].unsqueeze(1).to_broadcast([P, HEADS, HC]),
                        scalar=valid_s[:, ds(m, 1)],
                        in1=kvn_s[:, i * D:(i + 1) * D].rearrange("p (g c) -> p g c", c=HC),
                        op0=ALU.mult, op1=ALU.add)
                last.then_inc(S["kvh"], 1)

            prepare(0, 0)
            with dve.Fori(0, NKV // 2) as it:
                for b in range(RING):
                    prepare(RING * it + b + 1, b + 1)
                    finish(RING * it + b, b)
                    (center, scale)[b % 2](2 * it + b // 2)
            dve.wait_ge(S["kvs"], NKV + 2)
            own.step(V.tensor_copy(base_s[:, :], eoff_s[:, :]))
            for c, bank in enumerate((p_y, p_c)):
                last = V.scalar_tensor_tensor(out=kv_s[:, c, :], in0=bank[:, 0, :], scalar=1.0 / NODES,
                                              in1=hmask_s[:, c, :], op0=ALU.mult, op1=ALU.mult)
            last.then_inc(S["kvm"], 1)
            at = p_t[:, :, :].rearrange("p (c a) b -> p c (a b)", c=KD)
            dve.wait_ge(S["at"], 1)
            for c, a in enumerate((mean_s, t1_s)):
                o = 1 - c
                last = V.tensor_copy(a[:, o * P:(o + 1) * P], at[:, c, o * P:(o + 1) * P])
                last = V.tensor_tensor(a[:, c * P:(c + 1) * P], at[:, c, c * P:(c + 1) * P], id_s[:, :], ALU.add)
            last.then_inc(S["atc"], 1)
            dve.wait_ge(S["m1"], 1)
            V.tensor_copy(m1_s[:, :, :], p_h[0][:, :, :].rearrange("p (c a) b -> p c (a b)", c=2))
            V.tensor_tensor(c1_s[:, :], p_h[1][:, 1, 0:2], b1_s[:, :], ALU.add).then_inc(S["c1"], 1)
            with dve.Fori(NKV // 2, NI) as it:
                for b in range(RING):
                    prepare(RING * it + b + 1, b + 1)
                    finish(RING * it + b, b)
            dve.wait_ge(S["added"], NG + 1)

            with dve.Fori(0, NT) as p:
                own.step(V.tensor_scalar(c_s[:, 0:1], agg_s[:, ds(p, 1), D:D + 1].squeeze(1), 1.0, None, ALU.max))
                own.step(V.reciprocal(c_s[:, 1:2], c_s[:, 0:1]))
                V.tensor_scalar(mean_s[:, :], agg_s[:, ds(p, 1), 0:D].squeeze(1), c_s[:, 1:2], None, ALU.mult
                                ).then_inc(S["mean"], 1)
                dve.wait_ge(S["xr"], 16 * p + 16)
                dve.wait_ge(S["xnr"], 16 * p + 16)
                dve.wait_ge(S["gnn"], p + 2)
                own.step(V.tensor_tensor(t1_s[:, :], p_gnn, xnr_s[:, :], ALU.add))
                own.step(V.scalar_tensor_tensor(out=t2_s[:, :], in0=t1_s[:, :], scalar=0.0, in1=xr_s[:, :],
                                                op0=ALU.max, op1=ALU.add))
                dve.wait_ge(S["mix2"], p + 2)
                own.step(V.tensor_tensor(t3_s[:, :], p_y[:, 0, :], xnr_s[:, :], ALU.add))
                own.step(V.tensor_tensor(t4_s[:, :], t3_s[:, :], b2_s[:, :], ALU.add))
                V.tensor_tensor(x2_s[:, :], t2_s[:, :], t4_s[:, :], ALU.add).then_inc(S["x2"], 1)
                dve.wait_ge(S["x2"], p + 2)
                own.step(V.bn_stats(st_s[:, 0, :], x2_s[:, :]), True)
                own.step(V.bn_aggr(mv_s[:, 0, :], st_s[:, 0, :]))
                V.tensor_scalar(ve_s[:, 0:1], mv_s[:, 0, 1:2], EPS, None, ALU.add).then_inc(S["ve2"], 1)
                dve.wait_ge(S["sd2"], p + 1)
                own.step(V.reciprocal(rs_s[:, 0:1], sd_s[:, 0:1]))
                dve.wait_ge(S["xfst"], 16 * p + 16)
                V.tensor_scalar(xf_s[:, :], x2_s[:, :], mv_s[:, 0, 0:1], rs_s[:, 0:1], ALU.subtract, ALU.mult
                                ).then_inc(S["xf"], 1)
                dve.wait_ge(S["lg"], p + 1)
                own.step(V.reduce_max(rv_s[:, 0:1], p_c[:, 0, 0:E], AX))
                V.tensor_scalar(rv_s[:, 1:2], rv_s[:, 0:1], -1.0, None, ALU.mult).then_inc(S["mx"], 1)
                dve.wait_ge(S["ex"], p + 2)
                own.step(V.reciprocal(rv_s[:, 3:4], rv_s[:, 2:3]))
                own.step(V.tensor_scalar(rt_s[:, 1, :], rt_s[:, 0, :], rv_s[:, 3:4], None, ALU.mult), True)
                own.step(V.max(rt_s[:, 2, :], rt_s[:, 1, :]), True)
                own.step(V.max_index(ri_s[:, :], rt_s[:, 2, :], rt_s[:, 1, :]))
                own.step(V.tensor_tensor(rv_s[:, 4:5], rt_s[:, 2, 0:1], rt_s[:, 2, 1:2], ALU.add))
                own.step(V.reciprocal(rv_s[:, 5:6], rv_s[:, 4:5]))
                own.step(V.tensor_copy(rv_s[:, 6:8], ri_s[:, 0:2]))
                own.step(V.tensor_tensor(oh_s[:, :, :], iota_s[:, 0:E].unsqueeze(1).to_broadcast([P, TOPK, E]),
                                         rv_s[:, 6:8].unsqueeze(2).to_broadcast([P, TOPK, E]), ALU.is_equal))
                V.tensor_tensor(sel_s[:, :], oh_s[:, 0, :], oh_s[:, 1, :], ALU.add).then_inc(S["sel"], 1)
                dve.wait_ge(S["cnt"], p + 2)
                own.step(V.tensor_tensor(rt_s[:, 3, :], p_c[:, 0, E:2 * E], base_s[:, :], ALU.add))
                V.tensor_tensor(base_s[:, :], p_c[:, 0, 2 * E:3 * E], base_s[:, :], ALU.add)
                own.step(V.tensor_tensor(ohp_s[:, :, :], oh_s[:, :, :],
                                         rt_s[:, 3, :].unsqueeze(1).to_broadcast([P, TOPK, E]), ALU.mult))
                own.step(V.tensor_reduce(rv_s[:, 8:10], ohp_s[:, :, :], AX, ALU.add))
                dve.wait_ge(S["sc"], 32 * p + 16)
                V.tensor_copy(posi_s[:, :], rv_s[:, 8:10])
                V.tensor_scalar(pay_s[:, :, 0], tcol_s[:, NT:NT + 1].to_broadcast([P, TOPK]),
                                tcol_s[:, ds(p, 1)], None, ALU.add)
                V.tensor_scalar(pay_s[:, :, 1].bitcast(F32), rt_s[:, 2, 0:2], rv_s[:, 5:6], None, ALU.mult
                                ).then_inc(S["pay"], 1)
                dve.wait_ge(S["y"], p + 2)
                dve.wait_ge(S["ost"], 16 * p + 16)
                own.step(V.tensor_tensor(t1_s[:, :], p_y[:, 0, :], x2_s[:, :], ALU.add))
                V.tensor_tensor(o_s[:, :], t1_s[:, :], b2s_s[:, :], ALU.add).then_inc(S["o"], 1)
            own.step(V.tensor_tensor(ntf_s[:, 0, :], base_s[0:1, :], eoff_s[0:1, :], ALU.subtract))
            own.step(V.tensor_scalar(nti_s[:, 0, :], ntf_s[:, 0, :], float(P - 1), None, ALU.add))
            own.step(V.tensor_scalar(nti_s[:, 1, :], nti_s[:, 0, :], 7, None, ALU.arith_shift_right))
            own.step(V.tensor_copy(ntf_s[:, 1, :], nti_s[:, 1, :]))
            own.step(V.memset(ntf_s[:, 2, :], 1.0))
            own.step(V.tensor_tensor_scan(out=ntf_s[:, 3, :], data0=ntf_s[:, 2, :], data1=ntf_s[:, 1, :],
                                          initial=0.0, op0=ALU.mult, op1=ALU.add))
            own.step(V.memset(tabf_s[:, :, :], 0.0))
            step_no = iota_s[0:1, 0:P]
            for e in range(E - 1):
                end = ntf_s[:, 3, e:e + 1]
                own.step(V.tensor_scalar(tabf_s[:, 2, :], step_no, end, ntf_s[:, 1, e:e + 1], ALU.is_ge, ALU.mult))
                own.step(V.tensor_tensor(tabf_s[:, 1, :], tabf_s[:, 1, :], tabf_s[:, 2, :], ALU.add))
                own.step(V.scalar_tensor_tensor(out=tabf_s[:, 3, :], in0=step_no, scalar=end,
                                                in1=tabf_s[:, 0, :], op0=ALU.is_ge, op1=ALU.add))
                own.step(V.tensor_copy(tabf_s[:, 0, :], tabf_s[:, 3, :]))
            own.step(V.tensor_tensor(tabf_s[:, 2, :], step_no, tabf_s[:, 1, :], ALU.subtract))
            own.step(V.tensor_scalar(tabf_s[:, 2, :], tabf_s[:, 2, :], float(P), None, ALU.mult))
            own.step(V.tensor_copy(tabi_s[:, 0, :], tabf_s[:, 0, :]))
            V.tensor_tensor(tabi_s[:, 2, AHEAD:P], tabf_s[:, 0, AHEAD:P], tabf_s[:, 0, 0:P - AHEAD], ALU.is_equal)
            V.scalar_tensor_tensor(out=tabi_s[:, 1, :], in0=tabf_s[:, 0, :], scalar=float(NP),
                                   in1=tabf_s[:, 2, :], op0=ALU.mult, op1=ALU.add).then_inc(S["tab"], 1)

            def tokens(h, s):
                V.tensor_copy(gtok_s[h][:, :], slots_s[:, ds(s, 1), 0:1].squeeze(1)).then_inc(S[f"gtok{h}"], 1)

            def biases(h, s):
                e = dve.value_load(tabi_s[0:1, 0, ds(s, 1)], min_val=0, max_val=E - 1)
                own.step(V.tensor_copy(gate_s[h][:, :], slots_s[:, ds(s, 1), 1:2].squeeze(1).bitcast(F32)), True)
                own.step(V.tensor_scalar(gb2_s[h], b2p_s[:, ds(e, 1), :].squeeze(1), gate_s[h][:, :], None, ALU.mult),
                         True)
                V.tensor_copy(b1_h[h][:, :], b1p_s[:, ds(e, 1), :].squeeze(1)).then_inc(S[f"bias{h}"], 1)

            dve.wait_ge(S["tab"], 1)
            dve.wait_ge(S["bp"], 32)
            for h in range(2):
                dve.wait_ge(S[f"slots{h}"], 16)
            for h in range(2):
                tokens(h, h)
            for h in range(2):
                biases(h, h)
            with dve.Fori(0, STEPS // 2) as it:
                for h in range(2):
                    s = 2 * it + h
                    dve.wait_ge(S["const"], 3)
                    dve.wait_ge(S[f"slots{h}"], 16 * it + 32)
                    dve.wait_ge(S[f"xg{h}"], 16 * it + 16)
                    tokens(h, s + AHEAD)
                    dve.wait_ge(S["const"], 3)
                    dve.wait_ge(S["scat"], 16 * s + 16)
                    own.step(V.tensor_copy(stok_s[h][:, :], slots_s[:, ds(s, 1), 0:1].squeeze(1)))
                    dve.wait_ge(S["yy"], s + 1)
                    V.scalar_tensor_tensor(out=yg_s[h][:, :], in0=y_bank[h], scalar=gate_s[h][:, :], in1=gb2_s[h],
                                           op0=ALU.mult, op1=ALU.add).then_inc(S[f"yg{h}"], 1)
                    dve.wait_ge(S["const"], 3)
                    dve.wait_ge(S[f"yg{h}"], it + 2)
                    biases(h, s + AHEAD)

        @block.tensor
        def _(pe):
            mm = nc.tensor.matmul
            pe.wait_ge(S["wts"], WTS)
            pe.wait_ge(S["const"], 3)
            pe.wait_ge(S["span"], 1)
            for n in ("kvt", "proj", "kvs"):
                pe.sem_inc(S[n], 1)
            pe.sem_inc(S["pass_"], RING)
            xq = pe.alloc_register("extra_pe")
            pe.reg_mov(xq, 1)
            lo_r, hi_r = pe.alloc_register("lo_pe"), pe.alloc_register("hi_pe")

            def sums(b):
                for u in range(U):
                    m = mm(p_agg[b % 2], onehot[:, b % 2, u, :], ring[b][:, u, :], start=u == 0, stop=u == U - 1)
                return m

            def aggregate(it, b):
                g = RING * it + b
                hi = pe.value_load(span_s[0:1, ds(g, 1)], min_val=0, max_val=NT - 1)
                lo = pe.value_load(span_s[0:1, ds(g + NS, 1)], min_val=0, max_val=NT - 1)
                pe.reg_mov(lo_r, lo)
                pe.reg_mov(hi_r, hi)
                for u in range(U):
                    pe.wait_ge(s_row[b][u], 16 * it + 16)
                with pe.If_lt(lo_r, hi_r):
                    with pe.Fori(lo, hi):
                        pe.wait_ge(S["const"], 3)
                        pe.wait_ge(S["xoneh"], xq)
                        sums(b).then_inc(S["xpass"], 1)
                        pe.reg_add(xq, xq, 1)
                pe.wait_ge(S["oneh"], g + 1)
                sums(b).then_inc(S["pass_"], 1)

            def transpose(to, of):
                return nc.tensor.transpose(to, of, id_s[:, :])

            def project(m, h, it):
                pe.wait_ge(S[f"kvx{h}"], 16 * it + 16)
                pe.wait_ge(S["kvtc"], m + 1)
                for k in range(KD):
                    t = transpose(p_t[:, k, :], kvx_s[h][:, k * P:(k + 1) * P])
                t.then_inc(S["kvt"], 1)
                pe.wait_ge(S["kvtc"], m + 2)
                pe.wait_ge(S["cen"], m + 1)
                for k in range(KD):
                    mm(p_kv, xt_s[:, k, :], wkv_s[:, k, :], start=k == 0, stop=False)
                mm(p_kv, ones_s[0:1, :], bkv_s[:, :], start=False, stop=True).then_inc(S["proj"], 1)

            def k_v(m):
                pe.wait_ge(S["kvh"], m + 1)
                for c, bank in enumerate((p_y, p_c)):
                    t = mm(bank[:, 0, :], kvh_s[:, c * P:(c + 1) * P], kvh_s[:, D:], start=False, stop=False,
                           skip_group_check=True)
                t.then_inc(S["kvs"], 1)

            for bank in (p_y, p_c):
                mm(bank[:, 0, :], zero_s[:, 0:P], zero_s[:, :], start=True, stop=False, skip_group_check=True)

            def kv_iteration(it, first=False):
                aggregate(it, 0)
                project(2 * it, 0, it)
                aggregate(it, 1)
                if not first:
                    k_v(2 * it - 1)
                aggregate(it, 2)
                project(2 * it + 1, 1, it)
                aggregate(it, 3)
                k_v(2 * it)

            kv_iteration(0, True)
            with pe.Fori(1, NKV // 2) as it:
                kv_iteration(it)
            k_v(NKV - 1)
            for bank in (p_y, p_c):
                m = mm(bank[:, 0, :], zero_s[:, 0:P], zero_s[:, :], start=False, stop=True, skip_group_check=True)
            m.then_inc(S["kvs"], 1)
            pe.wait_ge(S["kvm"], 1)
            for c in range(KD):
                for k in range(KD):
                    m = mm(p_t[:, 2 * c:2 * c + 2, :].rearrange("p a b -> p (a b)"), kv_s[:, k, c * P:(c + 1) * P], wq_s[:, k, :], start=k == 0, stop=k == KD - 1)
            m.then_inc(S["at"], 1)
            for c in range(KD):
                for k in range(KD):
                    m = mm(p_h[1][:, 0, c:c + 1], kv_s[:, k, c * P:(c + 1) * P], bq_s[:, k:k + 1],
                           start=k == 0, stop=k == KD - 1)
            m.then_inc(S["bqk"], 1)
            pe.wait_ge(S["atc"], 1)
            at = (mean_s, t1_s)
            for c in range(KD):
                for k in range(KD):
                    mm(p_h[0][:, 2 * c:2 * c + 2, :].rearrange("p a b -> p (a b)"), at[k][:, c * P:(c + 1) * P], w1_s[:, k, :],
                       start=k == 0, stop=k == KD - 1)
            pe.wait_ge(S["bqc"], 1)
            for c in range(KD):
                for k in range(KD):
                    m = mm(p_h[1][:, 1, c:c + 1], w1_s[:, k, c * P:(c + 1) * P], c_s[:, k:k + 1],
                           start=k == 0, stop=k == KD - 1)
            m.then_inc(S["m1"], 1)
            with pe.Fori(NKV // 2, NI) as it:
                for b in range(RING):
                    aggregate(it, b)

            for n in ("mix1", "gnn", "mix2", "sage", "cnt", "y"):
                pe.sem_inc(S[n], 1)
            pe.wait_ge(S["c1"], 1)
            with pe.Fori(0, NT) as p:
                pe.wait_ge(S["xnr"], 16 * p + 16)
                pe.wait_ge(S["mean"], p + 1)
                pe.wait_ge(S["xfc"], p + 1)
                for k in range(KD):
                    transpose(p_t[:, k, :], xnr_s[:, k * P:(k + 1) * P])
                for k in range(KD):
                    m = transpose(p_t[:, 2 + k, :], mean_s[:, k * P:(k + 1) * P])
                m.then_inc(S["tm"], 1)
                pe.wait_ge(S["tc"], p + 2)
                pe.wait_ge(S["relu"], p + 1)
                pe.wait_ge(S["x2"], p + 1)
                for j in range(KD):
                    for k in range(KD):
                        mm(p_a[:, j, :], wl_s[:, k, j * P:(j + 1) * P], xt_s[:, 2 + k, :], start=k == 0, stop=False)
                    for k in range(KD):
                        m = mm(p_a[:, j, :], wr_s[:, k, j * P:(j + 1) * P], xt_s[:, k, :], start=False, stop=k == KD - 1)
                m.then_inc(S["sage"], 1)
                pe.wait_ge(S["gl"], p * KF + 1)
                for j in range(KD):
                    for k in range(KD):
                        m = mm(p_h[0][:, j, :], m1_s[:, k, j * P:(j + 1) * P], xt_s[:, k, :],
                               start=k == 0, stop=k == KD - 1)
                m.then_inc(S["mix1"], 1)
                pe.wait_ge(S["relu"], p + 2)
                for j in range(KD):
                    m = mm(p_gnn, act_s[:, j, :], wln_s[:, j, :], start=j == 0, stop=j == KD - 1)
                m.then_inc(S["gnn"], 1)
                pe.wait_ge(S["g1"], p + 2)
                pe.wait_ge(S["o"], p + 1)
                for j in range(KD):
                    m = mm(p_y[:, 0, :], act_s[:, 2 + j, :], w2_s[:, j, :], start=j == 0, stop=j == KD - 1)
                m.then_inc(S["mix2"], 1)
                pe.wait_ge(S["xf"], p + 1)
                for k in range(KD):
                    m = transpose(p_t[:, k, :], xf_s[:, k * P:(k + 1) * P])
                m.then_inc(S["txf"], 1)
                pe.wait_ge(S["xfc"], p + 2)
                for k in range(KD):
                    m = mm(p_c[:, 0, 0:E], xft_s[:, k, :], wrt_s[:, k, :], start=k == 0, stop=k == KD - 1)
                m.then_inc(S["lg"], 1)

                def up(j):
                    pe.wait_ge(S["gl"], p * KF + max(j - 1, 0) + 1)
                    for k in range(KD):
                        m = mm(p_h[j % 2][:, 0, :], w1s_s[:, k, j * P:(j + 1) * P], xft_s[:, k, :],
                               start=k == 0, stop=k == KD - 1)
                    m.then_inc(S["h"], 1)

                def down(j):
                    pe.wait_ge(S["gl"], p * KF + j + 2)
                    return mm(p_y[:, 0, :], hid_s[:, j, :], w2s_s[:, j, :], start=j == 0, stop=j == KF - 1)

                up(0)
                up(1)
                for j in range(KF):
                    m = down(j)
                    if j + 2 < KF:
                        up(j + 2)
                m.then_inc(S["y"], 1)
                pe.wait_ge(S["sel"], p + 1)
                mm(p_c[:, 0, E:2 * E], triu_s[:, :], sel_s[:, :], start=True, stop=True)
                mm(p_c[:, 0, 2 * E:3 * E], ones_s[:, :], sel_s[:, :], start=True, stop=True).then_inc(S["cnt"], 1)
            pe.wait_ge(S["w2p"], 16)
            pe.wait_ge(S["tab"], 1)

            def transposes(s, h, n):
                pe.wait_ge(S[f"xg{h}"], 16 * n)
                for k in range(KD):
                    m = transpose(p_t[:, k, :], xg_s[h][:, k * P:(k + 1) * P])
                m.then_inc(S["yt"], 1)

            def up(s, h, j):
                pe.wait_ge(S["ygl"], s * KF + j + 1)
                for k in range(KD):
                    m = mm(p_h[j % 2][:, 0, :], w1p_s[h][:, k, j * P:(j + 1) * P], yxt_s[h][:, k, :],
                           start=k == 0, stop=k == KD - 1)
                m.then_inc(S["yh"], 1)

            def ready(s, h, n):
                pe.wait_ge(S["ytc"], s + 1)
                pe.wait_ge(S[f"w1p{h}"], 16 * n)

            transposes(0, 0, 1)
            ready(0, 0, 1)
            up(0, 0, 0)
            up(0, 0, 1)
            with pe.Fori(0, STEPS // 2) as it:
                for h in range(2):
                    s = 2 * it + h
                    e = pe.value_load(tabi_s[0:1, 0, ds(s, 1)], min_val=0, max_val=E - 1)
                    pe.wait_ge(S[f"yg{h}"], it + 1)
                    for j in range(KF):
                        pe.wait_ge(S["ygl"], s * KF + j + 3)
                        m = mm(y_bank[h], hid_s[:, j, :], w2p_s[:, ds(e, 1), j, :].squeeze(1),
                               start=j == 0, stop=j == KF - 1)
                        if j == KF - 1:
                            m.then_inc(S["yy"], 1)
                        if j + 2 == KF:
                            ready(s + 1, 1 - h, it + 1 + h)
                        if j + 2 < KF:
                            up(s, h, j + 2)
                        else:
                            up(s + 1, 1 - h, j + 2 - KF)
                        if j == KF // 2 - 1:
                            transposes(s + 1, 1 - h, it + 1 + h)


_WEIGHTS = ["wl", "bl", "wr", "wln", "wkv", "bkv", "wq", "bq", "kvg", "kvb", "w1", "b1", "w2", "b2", "wrt",
            "w1s", "b1s", "w2s", "b2s", "w1p", "b1p", "w2p", "b2p"]
_CONSTS = ["ident", "triu", "valid", "iota", "tcol", "eoff", "hmask", "slot0"]


def kernel(**inputs):
    import numpy as np
    import concourse.bacc as bacc
    from concourse.bass_utils import run_bass_kernel_spmd as run

    v = {k: np.asarray(a) for k, a in inputs.items()}

    def by_rows(w):
        return w.reshape(w.shape[0] // P, P, -1).transpose(1, 0, 2)

    def column(b):
        return b.reshape(-1, P).T

    def wide(b):
        return np.broadcast_to(b.reshape(1, -1), (P, b.size))

    qkv = v["L0_mix_w_qkv"].reshape(D, HEADS, 3, HC)
    bqkv = v["L0_mix_b_qkv"].reshape(HEADS, 3, HC)
    x = np.zeros((NP, D), np.float32)
    x[:NODES] = v["x"]
    src = np.zeros((NG + RING) * U * P, np.int32)
    src[:EDGES] = v["src"]
    dst = np.full((NG + 1) * U * P, NP - 1, np.int32)
    dst[:EDGES] = v["dst"]
    slot0 = np.zeros((SLOTS, 2), np.int32)
    slot0[:, 0] = NP + np.arange(SLOTS) % P
    a = {
        "x": x,
        "idx": src.reshape(NG + RING, U, P).transpose(0, 2, 1),
        "dst": dst.reshape((NG + 1) * U, P).T,
        "wl": by_rows(v["L0_gnn_W_l"].T), "bl": column(v["L0_gnn_b_l"]),
        "wr": by_rows(v["L0_gnn_W_r"].T), "wln": by_rows(v["L0_gnn_W_ln"].T),
        "wkv": by_rows(np.concatenate([qkv[:, :, 1].reshape(D, D), qkv[:, :, 2].reshape(D, D)], 1)),
        "bkv": np.concatenate([bqkv[:, 1].reshape(1, D), bqkv[:, 2].reshape(1, D)], 1),
        "wq": by_rows(qkv[:, :, 0].reshape(D, D).T), "bq": column(bqkv[:, 0].reshape(D)),
        "kvg": wide(np.concatenate([v["L0_mix_kln_g"], v["L0_mix_vln_g"]])),
        "kvb": wide(np.concatenate([v["L0_mix_kln_b"], v["L0_mix_vln_b"]])),
        "w1": by_rows(v["L0_mix_w1"]), "b1": column(v["L0_mix_b1"]),
        "w2": by_rows(v["L0_mix_w2"]), "b2": wide(v["L0_mix_b2"]),
        "wrt": by_rows(v["L0_ffn_Wr"]),
        "w1s": by_rows(v["L0_ffn_W1s"]), "b1s": column(v["L0_ffn_b1s"]),
        "w2s": by_rows(v["L0_ffn_W2s"]), "b2s": wide(v["L0_ffn_b2s"]),
        "w1p": v["L0_ffn_W1p"], "b1p": v["L0_ffn_b1p"].reshape(E, KF, P).transpose(0, 2, 1),
        "w2p": v["L0_ffn_W2p"], "b2p": v["L0_ffn_b2p"],
        "ident": np.eye(P, dtype=np.float32),
        "triu": np.triu(np.ones((P, P), np.float32), 1),
        "valid": (np.arange(NKV * P).reshape(NKV, P).T < NODES).astype(np.float32),
        "iota": np.broadcast_to(np.arange(P, dtype=np.float32), (P, P)),
        "tcol": np.concatenate([np.broadcast_to(P * np.arange(NT, dtype=np.float32), (P, NT)),
                                np.arange(P, dtype=np.float32)[:, None]], 1),
        "eoff": np.broadcast_to(NP * np.arange(E, dtype=np.float32), (P, E)),
        "hmask": by_rows(np.kron(np.eye(HEADS, dtype=np.float32), np.ones((HC, HC), np.float32))),
        "slot0": slot0,
    }
    nc = bacc.Bacc("TRN2", target_bir_lowering=False, num_devices=1)
    arrays, args = {}, {}
    for name in ["x", "idx", "dst"] + _WEIGHTS + _CONSTS:
        arr = np.ascontiguousarray(a[name])
        arrays[f"in_{name}"] = arr
        args[name] = nc.dram_tensor(f"in_{name}", arr.shape, mybir.dt.from_np(arr.dtype), kind="ExternalInput").ap()
    out = nc.dram_tensor("out_rows", (PADROWS, D), F32, kind="ExternalOutput").ap()
    gps_layer(nc, out=out, **args)
    r = run(nc, [arrays], core_ids=[0])
    return r.results[0]["out_rows"][:NODES]
```

```python
import concourse.bass as bass
from concourse import mybir
from contextlib import ExitStack

F32 = mybir.dt.float32
I16 = mybir.dt.int16
I32 = mybir.dt.int32
U32 = mybir.dt.uint32
ALU = mybir.AluOpType
ACT = mybir.ActivationFunctionType
AX = mybir.AxisListType.X
RMAX = bass.bass_isa.ReduceOp.max
IND = bass.IndirectOffsetOnAxis
ds = bass.ds

P = 128
NODES, D = 6250, 256
EDGES = 200000
NT = -(-NODES // P)
NP = NT * P
KD = D // P
NKV = NT + NT % 2
U = 4
RING = 4
NI = -(-EDGES // (P * U * RING))
NG = NI * RING
HEADS, HC = 8, 32
NH2 = 2 * HEADS
F = 1024
KF = F // P
E, TOPK = 8, 2
STEPS = NT * TOPK + E
AHEAD = 2
LISTED = 2 * AHEAD
PADROWS = NP + P
SLOTS = (E - 1) * NP + (STEPS + LISTED - NT) * P
assert SLOTS % (2 * P) == 0
EPS = 1e-5
XCH = 7
RW = D + 2


def node_steps(eng, begin, step, plain):
    p_r, touched = eng.alloc_register("tile"), eng.alloc_register("touched")
    eng.reg_mov(p_r, 0)

    def both(edges):
        with eng.If_lt(p_r, 1):
            step(0, edges, second=False)
        with eng.Else():
            step(eng.snap(p_r, min_val=1, max_val=NT - 1), edges)
        eng.reg_add(p_r, p_r, 1)

    with eng.Fori(NKV // 2, NI) as it:
        edges = begin(it)
        eng.reg_mov(touched, edges[1])
        with eng.If_lt(p_r, touched):
            both(edges)
        with eng.Else():
            plain(edges)
    p = eng.snap(p_r, min_val=0, max_val=NT - 1)
    with eng.Fori(p, NT):
        both(None)
    step(NT, None, first=False)


class Word:

    def __init__(self, eng, row, most, name="word"):
        self.eng, self.row, self.most = eng, row, most
        self.word = eng.alloc_register(name)

    def look_up(self, it):
        self.eng.reg_mov(self.word, self.eng.value_load(self.row[:, ds(it, 1)], min_val=0, max_val=self.most))

    def now(self):
        return self.eng.snap(self.word, min_val=0, max_val=self.most)


class Own:

    def __init__(self, eng, sem, ready):
        self.eng, self.sem, self.ready = eng, sem, ready
        self.done = eng.alloc_register("own_done")
        eng.reg_mov(self.done, 0)

    def step(self, ins, constant_wait=False):
        ins.then_inc(self.sem, 1)
        self.eng.reg_add(self.done, self.done, 1)
        if constant_wait:
            self.eng.wait_ge(*self.ready)
        self.eng.wait_ge(self.sem, self.done)


def gps_layer(nc, x, idx, dst, wl, bl, wr, wln, wkv, bkv, wq, bq, kvg, kvb, w1, b1, w2, b2, wrt,
              w1s, b1s, w2s, b2s, w1p, b1p, w2p, b2p, ident, triu, valid, iota, tcol, eoff,
              hmask, slot0, out):
    ctx = ExitStack()
    with ctx:
        def sb(name, shape, dt=F32):
            return ctx.enter_context(nc.sbuf_tensor(name, shape, dt))

        def pb(name, shape):
            return ctx.enter_context(nc.psum_tensor(name, shape, F32))

        def sem(name):
            return ctx.enter_context(nc.semaphore(name))

        xn_d = nc.dram_tensor("xn_d", [NKV * P, D], F32, kind="Internal").ap()
        xf_d = nc.dram_tensor("xf_d", [PADROWS, D], F32, kind="Internal").ap()
        slot_d = nc.dram_tensor("slot_d", [SLOTS, 2], I32, kind="Internal").ap()

        id_s = sb("id_s", [P, P])
        triu_s = sb("triu_s", [P, P])
        ones_s = sb("ones_s", [P, P])
        zero_s = sb("zero_s", [P, D])
        valid_s = sb("valid_s", [P, NKV])
        iota_s = sb("iota_s", [P, P])
        tcol_s = sb("tcol_s", [P, NT + 1])
        eoff_s = sb("eoff_s", [P, E])
        wl_s = sb("wl_s", [P, KD, D])
        wr_s = sb("wr_s", [P, KD, D])
        wln_s = sb("wln_s", [P, KD, D])
        bl_s = sb("bl_s", [P, KD])
        wkv_s = sb("wkv_s", [P, KD, 2 * D])
        tabf_s = sb("tabf_s", [1, 5, P])
        bkv_s = tabf_s[:, 0:4, :].rearrange("p a b -> p (a b)")
        bq_s = sb("bq_s", [P, KD])
        kvg_s = sb("kvg_s", [P, 2 * HC])
        kvb_s = sb("kvb_s", [P, 2 * HC])
        w1_s = sb("w1_s", [P, KD, D])
        b1_s = sb("b1_s", [P, KD])
        w2_s = sb("w2_s", [P, KD, D])
        b2_s = sb("b2_s", [P, D])
        wrt_s = sb("wrt_s", [P, KD, E])
        w1s_s = sb("w1s_s", [P, KD, F])
        b1s_s = sb("b1s_s", [P, KF])
        w2s_s = sb("w2s_s", [P, KF, D])
        b2s_s = sb("b2s_s", [P, D])
        rows4 = sb("rows4", [P, 4, D])
        xr_s, x2_s, xf_s, o_s = (rows4[:, i, :] for i in range(4))
        hmask_s, wq_s = rows4[:, 0:2, :], rows4[:, 2:4, :]
        m1_s = sb("m1_s", [P, KD, D])
        c1_s = sb("c1_s", [P, KD])

        region = sb("region", [P, E * KF * D])
        x_s = region[:, 0:NT * D].rearrange("p (t d) -> p t d", d=D)
        w2p_s = region[:, :].rearrange("p (e j d) -> p e j d", e=E, d=D)
        late = sb("late", [P, NT * RW])
        agg_s = late[:, :].rearrange("p (t d) -> p t d", d=RW)

        dst_s = sb("dst_s", [P, (NG + 2) * U], I16)
        row_s = sb("row_s", [P, (NG + 2) * U], mybir.dt.uint8)
        upper_s = sb("upper_s", [P, NG + 1])
        lower_s = sb("lower_s", [P, 2])
        idx_s = [sb(f"idx_s{b}", [P, U], I32) for b in range(RING)]
        ring = [sb(f"ring{b}", [P, U, RW]) for b in range(RING)]
        onehot = sb("onehot", [P, 2, U, P])
        NS = NG + 1
        span_s = sb("span_s", [1, 2 * NS], I32)
        word_s = sb("word_s", [1, 3, NI + 1], I32)
        tile_i = onehot[:, :, :, :].rearrange("p a b c -> p (a b c)")[:, 0:2 * NS].bitcast(I32)

        w1p_s = [late[:, h * KD * F:(h + 1) * KD * F].rearrange("p (k f) -> p k f", f=F) for h in range(2)]
        after = 2 * KD * F
        xg_s, yg_s, gb2_s = ([late[:, after + (2 * i + h) * D:][:, 0:D] for h in range(2)] for i in range(3))
        after += 6 * D
        b2p_s = late[:, after:after + E * D].rearrange("p (e d) -> p e d", d=D)
        b1p_s = late[:, after + E * D:after + E * (D + KF)].rearrange("p (e j) -> p e j", j=KF)
        after += E * (D + KF)
        slots_s = late[:, after:after + 2 * (STEPS + LISTED)].bitcast(I32).rearrange("p (s w) -> p s w", w=2)
        tick_s = [late[0:1, after + 2 * (STEPS + LISTED) + h * KF:][:, 0:KF] for h in range(2)]
        gtok_s = [sb(f"gtok_s{h}", [P, 1], I32) for h in range(2)]
        stok_s = [sb(f"stok_s{h}", [P, 1], I32) for h in range(2)]
        gate_s = [sb(f"gate_s{h}", [P, 1]) for h in range(2)]
        b1_h = [sb(f"b1_h{h}", [P, KF]) for h in range(2)]
        work = sb("work", [P, 4, 2 * D])
        flat = work[:, :, :].rearrange("p a b -> p (a b)")
        dst32_s = flat[:, 0:(NG + 2) * U].bitcast(I32)
        ext_s, extr_s = flat[:, 0:2 * NS], flat[:, 2 * NS:4 * NS]
        cen_s, sq_s, kvn_s, kvh_s = (work[:, i, :] for i in range(4))
        hid_s = work[:, 0:2, :].rearrange("p a (b c) -> p (a b) c", c=P)
        t1_s, t2_s, t3_s, t4_s = (work[:, 2 + i // 2, i % 2 * D:(i % 2 + 1) * D] for i in range(4))
        xt_s = sb("xt_s", [P, 4, P])
        xft_s = sb("xft_s", [P, KD, P])
        yxt_s = (xft_s[:, :, :], xt_s[:, 0:KD, :])
        act_s = sb("act_s", [P, 4, P])
        kv_s = act_s[:, :, :].rearrange("p (c a) b -> p c (a b)", c=KD)

        xnr_s = sb("xnr_s", [P, D])
        mean_s = sb("mean_s", [P, D])
        st_s = sb("st_s", [P, XCH, 6])
        mv_s = sb("mv_s", [P, XCH, 2])
        ve_s = sb("ve_s", [P, NH2])
        sd_s = sb("sd_s", [P, NH2])
        rs_s = sb("rs_s", [P, NH2])
        hm_s = sb("hm_s", [P, NH2])
        c_s = sb("c_s", [P, 2])
        warm_s = sb("warm_s", [P, 1])
        rt_s = sb("rt_s", [P, 4, E])
        ri_s = sb("ri_s", [P, E], U32)
        oh_s = sb("oh_s", [P, TOPK, E])
        ohp_s = sb("ohp_s", [P, TOPK, E])
        sel_s = sb("sel_s", [P, E])
        base_s = sb("base_s", [P, E])
        rv_s = sb("rv_s", [P, 16])
        posi_s = sb("posi_s", [P, TOPK], I32)
        pay_s = sb("pay_s", [P, TOPK, 2], I32)
        tabi_s = sb("tabi_s", [1, 3, P], I32)
        nti_s = sb("nti_s", [1, 2, E], I32)
        ntf_s = sb("ntf_s", [1, 4, E])

        p_agg0 = pb("p_agg0", [P, 512])
        p_t = pb("p_t", [P, 4, P])
        p_a = pb("p_a", [P, 4, P])
        p_agg1 = pb("p_agg1", [P, 512])
        p_c = pb("p_c", [P, 2, D])
        p_h = [pb(f"p_h{i}", [P, 4, P]) for i in range(2)]
        p_y = pb("p_y", [P, 2, D])
        p_kv = p_a[:, :, :].rearrange("p a b -> p (a b)")

        kvx_s = (xnr_s, mean_s)
        p_agg = (p_agg0[:, 0:RW], p_agg1[:, 0:RW])
        p_mix, p_gnn = (p_a[:, i:i + 2, :].rearrange("p a b -> p (a b)") for i in (0, 2))
        y_bank = (p_y[:, 0, :], p_agg1[:, 0:D])

        WIDE, SEVERAL = 2 ** RING, 4 ** RING

        names = """wts const dstin xin xn xnst aggz ext extr span own_dve
            idx0 idx1 idx2 idx3 oneh pass_ added xoneh xpass
            kvx0 kvx1 kvt kvtc proj cen sq ssq ve sd kvh kvs kvm at atc bqk bqc m1 c1
            xr xnr mean tm tc sage mix1 relu g1 mix2 x2 ve2 sd2 xf xfst txf xfc lg h gl y o ost
            mx ex sel cnt pos pay sc tab w2p
            slots0 slots1 bp w1p0 w1p1 gtok0 gtok1 bias0 bias1 xg0 xg1 yt ytc yh ygl yy yg0 yg1 scat""".split()
        S = {n: sem(f"s_{n}") for n in names}
        s_row = [[sem(f"s_row{b}_{u}") for u in range(U)] for b in range(RING)]
        block = ctx.enter_context(nc.Block())

        def rows(ap, t, n=P):
            return ap[ds(t * n, n), :]

        loads = [(id_s[:, :], ident), (triu_s[:, :], triu), (valid_s[:, :], valid), (iota_s[:, :], iota),
                 (tcol_s[:, :], tcol), (eoff_s[:, :], eoff), (wl_s[:, :, :], wl),
                 (wr_s[:, :, :], wr), (wln_s[:, :, :], wln), (bl_s[:, :], bl), (wkv_s[:, :, :], wkv),
                 (bkv_s[:, :], bkv), (wq_s[:, :, :], wq), (bq_s[:, :], bq), (kvg_s[:, :], kvg),
                 (kvb_s[:, :], kvb), (w1_s[:, :, :], w1), (b1_s[:, :], b1), (w2_s[:, :, :], w2),
                 (b2_s[:, :], b2), (wrt_s[:, :, :], wrt), (w1s_s[:, :, :], w1s), (b1s_s[:, :], b1s),
                 (w2s_s[:, :, :], w2s), (b2s_s[:, :], b2s), (hmask_s[:, :, :], hmask)]
        WTS = 16 * (len(loads) + 1)

        @block.sync
        def _(sp):
            sp.dma_start(dst32_s, dst).then_inc(S["dstin"], 16)
            for c in range(NT // XCH):
                if c:
                    sp.wait_ge(S["xin"], 16 * c)
                sp.dma_start(x_s[:, c * XCH:(c + 1) * XCH, :],
                             x[c * XCH * P:(c + 1) * XCH * P, :].rearrange("(t p) d -> p t d", p=P)
                             ).then_inc(S["xin"], 16)
            for to, of in loads:
                sp.dma_start(to, of).then_inc(S["wts"], 16)
            sp.wait_ge(S["const"], 3)
            sp.dma_start(xf_d[NP:PADROWS, :], zero_s[:, :]).then_inc(S["xfst"], 16)
            sp.dma_start(out[NP:NP + P // 2, :], zero_s[0:P // 2, :]).then_inc(S["ost"], 16)
            sp.dma_start(xn_d[NT * P:NKV * P, :], zero_s[:, :]).then_inc(S["wts"], 16)
            sp.wait_ge(S["xnst"], 16 * (NT // XCH))
            sp.dma_start(w2p_s, w2p.rearrange("e (j p) d -> p e j d", p=P)).then_inc(S["w2p"], 16)

            def load_idx(b, it):
                sp.dma_start(idx_s[b][:, :], idx[ds(RING * it + b, 1), :, :].squeeze(0)).then_inc(S[f"idx{b}"], 16)

            def next_idx(b, it):
                for u in range(U):
                    sp.wait_ge(s_row[b][u], 16 * it + 16)
                load_idx(b, it + 1)

            def load_kvx(h, it):
                sp.dma_start(kvx_s[h][:, :], rows(xn_d, 2 * it + h)).then_inc(S[f"kvx{h}"], 16)

            for b in range(RING):
                load_idx(b, 0)
            for h in range(2):
                load_kvx(h, 0)
            sp.wait_ge(S["span"], 2)
            with sp.Fori(0, NKV // 2 - 1) as it:
                for b in range(RING):
                    next_idx(b, it)
                    if b % 2 == 0:
                        sp.wait_ge(S["kvt"], 2 * it + b // 2 + 2)
                        load_kvx(b // 2, it + 1)
            with sp.Fori(NKV // 2 - 1, NKV // 2) as it:
                for b in range(RING):
                    next_idx(b, it)

            def step(p, edges, first=True, second=True):
                if first:
                    sp.wait_ge(S["x2"], p + 1)
                    sp.dma_start(xr_s[:, :], rows(x, p)).then_inc(S["xr"], 16)
                    sp.dma_start(xnr_s[:, :], rows(xn_d, p)).then_inc(S["xnr"], 16)
                if second:
                    sp.wait_ge(S["xf"], p)
                    sp.dma_start(rows(xf_d, p - 1), xf_s[:, :]).then_inc(S["xfst"], 16)
                if edges is not None:
                    plain(edges)
                if second:
                    sp.wait_ge(S["o"], p + 1)
                    sp.dma_start(rows(out, p - 1), o_s[:, :]).then_inc(S["ost"], 16)

            def plain(edges):
                for b in range(RING):
                    next_idx(b, edges[0])
                    if b == 0:
                        word.look_up(edges[0] + 1)

            sp.wait_ge(S["c1"], 1)
            word = Word(sp, word_s[0:1, 0, :], WIDE * NT - 1)
            word.look_up(NKV // 2)
            node_steps(sp, lambda it: (it, word.now() >> RING), step, plain)
            sp.wait_ge(S["tab"], 1)
            sp.wait_ge(S["sc"], 16 * (2 * NT + 2))
            sp.dma_start(b1p_s, b1p.rearrange("e p j -> p e j")).then_inc(S["bp"], 16)
            sp.dma_start(b2p_s, b2p.unsqueeze(0).to_broadcast([P, E, D])).then_inc(S["bp"], 16)

            flag = sp.alloc_register("flag")

            def load_w1p(h, s):
                e = sp.value_load(tabi_s[0:1, 0, ds(s, 1)], min_val=0, max_val=E - 1)
                sp.dma_start(w1p_s[h][:, :, :], w1p[ds(e, 1), :, :].squeeze(0).rearrange("(k p) f -> p k f", p=P)
                             ).then_inc(S[f"w1p{h}"], 16)

            def load_slots(h, s):
                o = sp.value_load(tabi_s[0:1, 1, ds(s, 1)], min_val=0, max_val=SLOTS - P)
                sp.dma_start(slots_s[:, ds(s, 1), :].squeeze(1), slot_d[ds(o, P), :]).then_inc(S[f"slots{h}"], 16)

            for h in range(2):
                load_slots(h, h)
            for h in range(2):
                load_w1p(h, h)
            for h in range(2):
                sp.wait_ge(S[f"slots{h}"], 16)
                load_slots(h, h + 2)
            with sp.Fori(0, STEPS // 2) as it:
                for h in range(2):
                    s = 2 * it + h
                    sp.wait_ge(S[f"slots{h}"], 16 * it + 32)
                    load_slots(h, s + LISTED)
                    same = sp.value_load(tabi_s[0:1, 2, ds(s + AHEAD, 1)], min_val=0, max_val=1)
                    sp.reg_mov(flag, same)
                    with sp.If_lt(flag, 1):
                        sp.wait_ge(S["yh"], s * KF + KF)
                        load_w1p(h, s + AHEAD)
                    with sp.Else():
                        sp.wait_ge(S["yh"], s * KF + KF)
                        sp.dma_start(tick_s[h], w1p[0, 0:1, 0:KF]).then_inc(S[f"w1p{h}"], 16)
            for h in range(2):
                sp.wait_ge(S[f"w1p{h}"], 16 * (STEPS // 2 + 1))
                sp.wait_ge(S[f"slots{h}"], 16 * (STEPS // 2 + 2))

        @block.gpsimd
        def _(pool):
            nc.gpsimd.memset(ones_s[:, :], 1.0).then_inc(S["const"], 1)
            nc.gpsimd.memset(zero_s[:, :], 0.0).then_inc(S["const"], 1)
            for b in range(RING):
                last = nc.gpsimd.memset(ring[b][:, :, D:RW], 1.0)
            last.then_inc(S["const"], 1)
            for i in range(2):
                half = slice(i * (SLOTS // 2), (i + 1) * (SLOTS // 2))
                pool.dma_start(slot_d[half, :].rearrange("(p c) w -> p (c w)", p=P),
                               slot0[half, :].rearrange("(p c) w -> p (c w)", p=P)).then_inc(S["sc"], 16)
            pool.wait_ge(S["const"], 3)
            for i in (2, 3):
                pool.dma_start(out[NP + i * P // 4:NP + (i + 1) * P // 4, :], zero_s[0:P // 4, :]
                               ).then_inc(S["scat"], 16)
            nc.gpsimd.memset(agg_s[:, :, :], 0.0).then_inc(S["aggz"], 1)
            pool.wait_ge(S["ext"], 1)
            nc.gpsimd.partition_all_reduce(extr_s[:, :], ext_s[:, :], P, RMAX).then_inc(S["extr"], 1)
            pool.wait_ge(S["xnst"], 16 * (NT // XCH))
            turn = pool.alloc_register("turn")
            turn16 = pool.alloc_register("turn16")
            group = pool.alloc_register("group")
            pool.reg_mov(group, 1)
            pool.reg_mov(turn16, 16)

            def gather_edges(b):
                pool.wait_ge(S["const"], 3)
                pool.wait_ge(S[f"idx{b}"], turn16)
                pool.wait_ge(S["pass_"], group)
                for u in range(U):
                    pool.indirect_dma_start(
                        out=ring[b][:, u, 0:D], out_offset=None, in_=xn_d,
                        in_offset=IND(ap=idx_s[b][:, u:u + 1], axis=0)).then_inc(s_row[b][u], 16)
                pool.reg_add(group, group, 1)

            def plain(edges):
                for b in range(RING):
                    gather_edges(b)
                pool.reg_add(turn16, turn16, 16)

            with pool.Fori(0, NKV // 2) as it:
                plain((it,))

            def next_edges(edges):
                word.look_up(edges[0] + 1)
                plain(edges)

            def scatter_slots():
                pool.wait_ge(S["const"], 3)
                pool.wait_ge(S["pay"], turn)
                for k in range(TOPK):
                    pool.indirect_dma_start(out=slot_d, out_offset=IND(ap=posi_s[:, k:k + 1], axis=0),
                                            in_=pay_s[:, k, :], in_offset=None).then_inc(S["sc"], 16)

            def step(p, edges, first=True, second=True):
                if edges is not None:
                    word.look_up(edges[0] + 1)
                for b in range(RING):
                    if edges is not None:
                        gather_edges(b)
                    if b == 2 and second:
                        with pool.If_lt(one, turn):
                            scatter_slots()
                if edges is not None:
                    pool.reg_add(turn16, turn16, 16)
                pool.reg_add(turn, turn, 1)

            pool.wait_ge(S["sc"], 32)
            pool.reg_mov(turn, 0)
            one = pool.alloc_register("one")
            pool.reg_mov(one, 1)
            pool.wait_ge(S["span"], 2)
            word = Word(pool, word_s[0:1, 0, :], WIDE * NT - 1)
            word.look_up(NKV // 2)
            node_steps(pool, lambda it: (it, word.now() >> RING), step, next_edges)
            scatter_slots()
            pool.wait_ge(S["xfst"], 16 * NT + 16)
            pool.wait_ge(S["ost"], 16 * NT + 16)

            def gather(h):
                pool.indirect_dma_start(out=xg_s[h][:, :], out_offset=None, in_=xf_d,
                                        in_offset=IND(ap=gtok_s[h][:, 0:1], axis=0)).then_inc(S[f"xg{h}"], 16)

            for h in range(2):
                pool.wait_ge(S[f"gtok{h}"], 1)
                gather(h)
            turn2 = pool.alloc_register("turn2")
            pool.reg_mov(turn2, 2)
            tile1 = pool.alloc_register("tile1")
            pool.reg_mov(tile1, 1)
            done16 = pool.alloc_register("done16")
            pool.reg_mov(done16, 32)
            with pool.Fori(0, STEPS // 2) as it:
                for h in range(2):
                    pool.wait_ge(S["const"], 3)
                    pool.wait_ge(S[f"gtok{h}"], turn2)
                    pool.wait_ge(S["yt"], tile1)
                    gather(h)
                    pool.wait_ge(S["const"], 3)
                    pool.wait_ge(S[f"yg{h}"], turn2)
                    pool.wait_ge(S["scat"], done16)
                    pool.indirect_dma_start(out=out, out_offset=IND(ap=stok_s[h][:, 0:1], axis=0),
                                            in_=yg_s[h][:, :], in_offset=None, compute_op=ALU.add
                                            ).then_inc(S["scat"], 16)
                    pool.reg_add(done16, done16, 16)
                    pool.reg_add(tile1, tile1, 1)
                pool.reg_add(turn2, turn2, 1)
            pool.wait_ge(S["scat"], 16 * STEPS + 32)
            for h in range(2):
                pool.wait_ge(S[f"xg{h}"], 16 * (STEPS // 2 + 1))

        @block.scalar
        def _(act):
            for n in ("kvtc", "sq"):
                act.sem_inc(S[n], 1)
            with act.Fori(0, NT // XCH) as c:
                act.wait_ge(S["ve"], c + 1)
                nc.scalar.activation(sd_s[:, 0:XCH], ve_s[:, 0:XCH], ACT.Sqrt).then_inc(S["sd"], 1)
                act.wait_ge(S["xn"], c + 1)
                act.dma_start(xn_d[ds(c * (XCH * P), XCH * P), :].rearrange("(t p) d -> p t d", p=P),
                              x_s[:, ds(c * XCH, XCH), :]).then_inc(S["xnst"], 16)
            with act.Fori(0, NKV) as m:
                act.wait_ge(S["kvt"], m + 2)
                act.wait_ge(S["proj"], m + 1)
                nc.scalar.activation(xt_s[:, 0:2, :], p_t[:, 0:2, :], ACT.Copy).then_inc(S["kvtc"], 1)
                act.wait_ge(S["cen"], m + 2)
                nc.scalar.activation(sq_s[:, :], cen_s[:, :], ACT.Square).then_inc(S["sq"], 1)
                act.wait_ge(S["ve"], m + NT // XCH + 1)
                nc.scalar.activation(sd_s[:, :], ve_s[:, :], ACT.Sqrt).then_inc(S["sd"], 1)
            act.wait_ge(S["bqk"], 1)
            nc.scalar.activation(c_s[:, 0:2], p_h[1][:, 0, 0:2], ACT.Copy).then_inc(S["bqc"], 1)
            for n in ("tc", "relu", "g1"):
                act.sem_inc(S[n], 1)
            act.sem_inc(S["gl"], KF + 1)

            def step(p, edges, first=True, second=True):
                def gelus(*js):
                    for j in js if second else ():
                        act.wait_ge(S["h"], p * KF + j + 1)
                        nc.scalar.activation(hid_s[:, j, :], p_h[(j + 1) % 2][:, 0, :], ACT.Gelu,
                                             bias=b1s_s[:, j:j + 1]).then_inc(S["gl"], 1)

                nc.scalar.activation(warm_s[:, :], zero_s[:, 0:1], ACT.Gelu)
                if second:
                    act.wait_ge(S["txf"], p)
                    act.wait_ge(S["y"], p)
                    nc.scalar.activation(xft_s[:, :, :], p_h[1][:, 2:4, :], ACT.Copy).then_inc(S["xfc"], 1)
                gelus(0, 1)
                if first:
                    act.wait_ge(S["tm"], p + 1)
                    act.wait_ge(S["mix2"], p + 1)
                    nc.scalar.activation(xt_s[:, :, :], p_t[:, :, :], ACT.Copy).then_inc(S["tc"], 1)
                gelus(2, 3)
                if first:
                    act.wait_ge(S["sage"], p + 1)
                    for j in range(KD):
                        r = nc.scalar.activation(act_s[:, j, :], p_a[:, j, :], ACT.Relu, bias=bl_s[:, j:j + 1])
                    r.then_inc(S["relu"], 1)
                gelus(4)
                if first:
                    act.wait_ge(S["mix1"], p + 1)
                    for j in range(KD):
                        r = nc.scalar.activation(act_s[:, 2 + j, :], p_c[:, 1, j * P:(j + 1) * P], ACT.Gelu,
                                                 bias=c1_s[:, j:j + 1])
                    r.then_inc(S["g1"], 1)
                gelus(5, 6)
                if edges is not None:
                    word.look_up(edges[0] + 1)
                gelus(7)
                if second:
                    act.wait_ge(S["mx"], p)
                    nc.scalar.activation(rv_s[:, 1:2], rv_s[:, 0:1], ACT.Exp).then_inc(S["ex"], 1)
                if first:
                    act.wait_ge(S["ve2"], p + 1)
                    nc.scalar.activation(sd_s[:, 0:1], ve_s[:, 0:1], ACT.Sqrt).then_inc(S["sd2"], 1)

            act.wait_ge(S["span"], 2)
            word = Word(act, word_s[0:1, 0, :], WIDE * NT - 1)
            word.look_up(NKV // 2)
            node_steps(act, lambda it: (it, word.now() >> RING), step, lambda edges: word.look_up(edges[0] + 1))
            act.sem_inc(S["ygl"], 2)

            def copy_xt(s, h):
                act.wait_ge(S["yt"], s + 1)
                nc.scalar.activation(yxt_s[h], p_t[:, 0:KD, :], ACT.Copy).then_inc(S["ytc"], 1)

            copy_xt(0, 0)
            with act.Fori(0, STEPS // 2) as it:
                for h in range(2):
                    s = 2 * it + h
                    act.wait_ge(S[f"bias{h}"], it + 1)
                    for j in range(KF):
                        act.wait_ge(S["yh"], s * KF + j + 1)
                        nc.scalar.activation(hid_s[:, j, :], p_h[j % 2][:, 0, :], ACT.Gelu,
                                             bias=b1_h[h][:, j:j + 1]).then_inc(S["ygl"], 1)
                        if j == KF // 2:
                            copy_xt(s + 1, 1 - h)

        @block.vector
        def _(dve):
            V = nc.vector
            own = Own(dve, S["own_dve"], (S["const"], 3))
            for n in ("cen", "ssq", "x2", "o", "pos", "pay", "yg0", "yg1"):
                dve.sem_inc(S[n], 1)
            dve.wait_ge(S["dstin"], 16)
            own.step(V.tensor_copy(dst_s[:, :], dst32_s))
            own.step(V.tensor_scalar(dst32_s, dst32_s, P - 1, None, ALU.bitwise_and))
            own.step(V.tensor_copy(row_s[:, :], dst32_s))
            own.step(V.tensor_reduce(ext_s[:, 0:NS], dst_s[:, 0:NS * U].rearrange("p (g u) -> p g u", u=U), AX, ALU.max))
            own.step(V.tensor_reduce(ext_s[:, NS:], dst_s[:, 0:NS * U].rearrange("p (g u) -> p g u", u=U), AX, ALU.min))
            V.tensor_scalar(ext_s[:, NS:], ext_s[:, NS:], -1.0, None, ALU.mult).then_inc(S["ext"], 1)
            with dve.Fori(0, NT // XCH) as c:
                dve.wait_ge(S["xin"], 16 * c + 16)
                for j in range(XCH):
                    i = V.bn_stats(st_s[:, j, :], x_s[:, ds(c * XCH + j, 1), :])
                own.step(i, True)
                for j in range(XCH):
                    i = V.bn_aggr(mv_s[:, j, :], st_s[:, j, :])
                own.step(i)
                V.tensor_scalar(ve_s[:, 0:XCH], mv_s[:, :, 1:2].squeeze(2), EPS, None, ALU.add).then_inc(S["ve"], 1)
                dve.wait_ge(S["sd"], c + 1)
                own.step(V.reciprocal(rs_s[:, 0:XCH], sd_s[:, 0:XCH]))
                for j in range(XCH):
                    xj = x_s[:, ds(c * XCH + j, 1), :]
                    i = V.tensor_scalar(xj, xj, mv_s[:, j, 0:1], rs_s[:, j:j + 1], ALU.subtract, ALU.mult)
                i.then_inc(S["xn"], 1)
            dve.wait_ge(S["wts"], WTS)
            dve.wait_ge(S["extr"], 1)
            own.step(V.tensor_copy(tile_i[:, 0:NS], extr_s[:, 0:NS]))
            own.step(V.tensor_scalar(tile_i[:, NS:], extr_s[:, NS:], -1.0, None, ALU.mult))
            own.step(V.tensor_scalar(ext_s[:, 0:NS].bitcast(I32), tile_i[:, 0:NS], P - 1, None, ALU.bitwise_and))
            own.step(V.tensor_copy(upper_s[:, :], ext_s[:, 0:NS].bitcast(I32)))
            own.step(V.tensor_scalar(upper_s[:, :], upper_s[:, :], tcol_s[:, NT:NT + 1], None, ALU.is_ge))
            own.step(V.tensor_tensor(ext_s[0:1, NS:], extr_s[0:1, 0:NS], extr_s[0:1, NS:], ALU.add))
            own.step(V.tensor_scalar(ext_s[0:1, NS:], ext_s[0:1, NS:], float(P), None, ALU.is_ge))
            V.tensor_scalar(span_s[0:1, :], tile_i[0:1, :], 7, None, ALU.arith_shift_right).then_inc(S["span"], 1)
            dve.sem_inc(S["added"], 1)
            touch, other, word, spare_s = (extr_s[0:1, i * P:i * P + NI] for i in range(4))
            flag_s, wide_f = ext_s[0:1, 0:NS], ext_s[0:1, NS:]
            dve.wait_ge(S["span"], 1)
            own.step(V.tensor_reduce(touch, span_s[0:1, NS:NS + NG].rearrange("p (i b) -> p i b", b=RING), AX, ALU.min))
            n = 1
            while n < NI:
                V.tensor_tensor(other[:, 0:NI - n], touch[:, 0:NI - n], touch[:, n:NI], ALU.min)
                own.step(V.tensor_copy(other[:, NI - n:NI], touch[:, NI - n:NI]))
                touch, other, n = other, touch, 2 * n
            own.step(V.tensor_scalar(other, touch, float(NT - 1), float(WIDE), ALU.min, ALU.mult))
            own.step(V.tensor_tensor(flag_s, span_s[0:1, 0:NS], span_s[0:1, NS:], ALU.is_gt))

            def pack(row, total, spare, terms):
                terms = [(source[0:1, shift:shift + NG].rearrange("p (i b) -> p b i", b=RING)[:, b, :],
                          float(first * base ** b)) for source, shift, first, base in terms for b in range(RING)]
                for i, (part, factor) in enumerate(terms):
                    to = word_s[:, row, 0:NI] if i == len(terms) - 1 else spare
                    own.step(V.scalar_tensor_tensor(out=to, in0=part, scalar=factor, in1=total,
                                                    op0=ALU.mult, op1=ALU.add))
                    total, spare = spare, total

            own.step(V.tensor_copy(word, other))
            pack(0, word, spare_s, [(wide_f, 0, 1, 2)])
            own.step(V.tensor_scalar(word, other, float(WIDE), None, ALU.mult))
            pack(1, word, spare_s, [(wide_f, 1, 1, 2), (flag_s, 1, WIDE, 2)])
            own.step(V.memset(word, 0.0))
            pack(2, word, spare_s, [(span_s, 1, 1, 64)])
            V.memset(word_s[:, :, NI:], 0.0).then_inc(S["span"], 1)
            xq = dve.alloc_register("extra_dve")
            dve.reg_mov(xq, 1)
            dve.wait_ge(S["span"], 2)
            dve.wait_ge(S["aggz"], 1)

            def hot(g, b, t=None):
                out, rows = onehot[:, b % 2, :, :], iota_s[:, :].unsqueeze(1).to_broadcast([P, U, P])
                to = (row_s if t is None else dst_s)[:, ds(g * U, U)].unsqueeze(2).to_broadcast([P, U, P])
                if t is None:
                    return V.tensor_tensor(out, to, rows, ALU.is_equal)
                return V.scalar_tensor_tensor(out=out, in0=to, scalar=tcol_s[:, ds(t, 1)], in1=rows,
                                              op0=ALU.subtract, op1=ALU.is_equal)

            def add(b, t):
                a = agg_s[:, ds(t, 1), :]
                return V.tensor_tensor(a, a, p_agg[b % 2].unsqueeze(1), ALU.add)

            wide = dve.alloc_register("wide_dve")
            several = [dve.alloc_register(f"several{i}") for i in range(2)]
            last_r = dve.alloc_register("last_tile")

            word = Word(dve, word_s[0:1, 1, :], SEVERAL * NT - 1)
            tiles = Word(dve, word_s[0:1, 2, :], 64 ** RING - 1, "last_tiles")

            def look_up(it):
                word.look_up(it)
                tiles.look_up(it)

            def begin(it):
                bits = word.now()
                return it, bits >> (2 * RING), bits, tiles.now(), [dve.snap(last_r, min_val=0, max_val=NT - 1)]

            def extra(g, b, hi):
                lo = dve.value_load(span_s[0:1, ds(g + NS, 1)], min_val=0, max_val=NT - 1)
                with dve.Fori(lo, hi) as t:
                    t = dve.snap(t, min_val=0, max_val=NT - 1)
                    hot(g, b, t).then_inc(S["xoneh"], 1)
                    dve.wait_ge(S["const"], 3)
                    dve.wait_ge(S["xpass"], xq)
                    own.step(add(b, t))
                    dve.reg_add(xq, xq, 1)

            def prepare(edges, b, later=False):
                it, _, bits, tiles, last = edges
                dve.reg_mov(several[b % 2], (bits >> (RING + b - 1)) & 1)
                last.append(dve.snap((tiles >> (6 * (b - 1))) & 63).with_bounds(min_val=0, max_val=NT - 1))
                if b == RING:
                    dve.reg_mov(last_r, last[b])
                dve.reg_mov(wide, (bits >> (b - 1)) & 1)
                if b > 1:
                    with dve.If_eq(wide, 0):
                        hot(RING * it + b, b).then_inc(S["oneh"], 1)
                if not later:
                    prepare_rest(edges, b)

            def prepare_rest(edges, b):
                g = RING * edges[0] + b
                with dve.If_eq(wide, 1):
                    extra(g, b, edges[4][b])
                    hot(g, b, edges[4][b]).then_inc(S["oneh"], 1)

            def prepare_next(g):
                dve.reg_mov(wide, word.word)
                dve.reg_mov(wide, dve.snap(wide, min_val=0, max_val=SEVERAL * NT - 1) & 1)
                with dve.If_eq(wide, 0):
                    hot(g, 1).then_inc(S["oneh"], 1)

            def finish(edges, b):
                it, _, bits, tiles, last = edges
                g = RING * it + b
                def ready():
                    dve.wait_ge(S["const"], 3)
                    dve.wait_ge(S["pass_"], g + RING + 1)
                    dve.wait_ge(S["added"], g + 1)

                with dve.If_eq(several[b % 2], 0):
                    ready()
                    add(b, last[b]).then_inc(S["added"], 1)
                with dve.Else():
                    ready()
                    a = agg_s[:, ds(last[b], 1), :].squeeze(1)
                    V.scalar_tensor_tensor(out=a, in0=p_agg[b % 2], scalar=upper_s[:, ds(g, 1)], in1=a,
                                           op0=ALU.mult, op1=ALU.add)
                    own.step(V.tensor_scalar(lower_s[:, 0:1], upper_s[:, ds(g, 1)], -1.0, 1.0, ALU.mult, ALU.add))
                    t = dve.snap(last[b] - 1).with_bounds(min_val=0, max_val=NT - 1)
                    a = agg_s[:, ds(t, 1), :].squeeze(1)
                    V.scalar_tensor_tensor(out=a, in0=p_agg[b % 2], scalar=lower_s[:, 0:1], in1=a,
                                           op0=ALU.mult, op1=ALU.add).then_inc(S["added"], 1)

            def center(m):
                dve.wait_ge(S["proj"], m + 2)
                kv3 = p_kv.rearrange("p (g c) -> p g c", c=HC)
                own.step(V.tensor_reduce(hm_s[:, :], kv3, AX, ALU.add))
                own.step(V.tensor_scalar(hm_s[:, :], hm_s[:, :], 1.0 / HC, None, ALU.mult))
                V.tensor_tensor(cen_s[:, :].rearrange("p (g c) -> p g c", c=HC), kv3,
                                hm_s[:, :].unsqueeze(2).to_broadcast([P, NH2, HC]), ALU.subtract).then_inc(S["cen"], 1)
                dve.wait_ge(S["sq"], m + 2)
                V.tensor_reduce(ve_s[:, :], sq_s[:, :].rearrange("p (g c) -> p g c", c=HC), AX, ALU.add
                                ).then_inc(S["ssq"], 1)
                dve.wait_ge(S["ssq"], m + 2)
                V.tensor_scalar(ve_s[:, :], ve_s[:, :], 1.0 / HC, EPS, ALU.mult, ALU.add).then_inc(S["ve"], 1)

            def scale(m):
                dve.wait_ge(S["sd"], m + NT // XCH + 1)
                own.step(V.reciprocal(rs_s[:, :], sd_s[:, :]))
                own.step(V.tensor_scalar(rs_s[:, :], rs_s[:, :], valid_s[:, ds(m, 1)], None, ALU.mult))
                own.step(V.tensor_tensor(kvn_s[:, :].rearrange("p (g c) -> p g c", c=HC),
                                         cen_s[:, :].rearrange("p (g c) -> p g c", c=HC),
                                         rs_s[:, :].unsqueeze(2).to_broadcast([P, NH2, HC]), ALU.mult))
                for i in range(2):
                    part = kvn_s[:, i * D:(i + 1) * D].rearrange("p (g c) -> p g c", c=HC)
                    last = V.tensor_tensor(part, part, kvg_s[:, i * HC:(i + 1) * HC].unsqueeze(1).to_broadcast([P, HEADS, HC]), ALU.mult)
                own.step(last)
                dve.wait_ge(S["kvs"], m + 1)
                for i in range(2):
                    last = V.scalar_tensor_tensor(
                        out=kvh_s[:, i * D:(i + 1) * D].rearrange("p (g c) -> p g c", c=HC),
                        in0=kvb_s[:, i * HC:(i + 1) * HC].unsqueeze(1).to_broadcast([P, HEADS, HC]),
                        scalar=valid_s[:, ds(m, 1)],
                        in1=kvn_s[:, i * D:(i + 1) * D].rearrange("p (g c) -> p g c", c=HC),
                        op0=ALU.mult, op1=ALU.add)
                last.then_inc(S["kvh"], 1)

            hi = dve.value_load(span_s[0:1, 0:1], min_val=0, max_val=NT - 1)
            lo = dve.value_load(span_s[0:1, NS:NS + 1], min_val=0, max_val=NT - 1)
            dve.reg_mov(last_r, hi)
            dve.reg_mov(several[0], lo)
            with dve.If_lt(several[0], last_r):
                extra(0, 0, hi)
            dve.reg_mov(several[0], 0)
            hot(0, 0, hi).then_inc(S["oneh"], 1)
            look_up(0)
            prepare_next(1)

            def kv_iteration(it, first=False):
                edges = begin(it)
                prepare(edges, 1)
                finish(edges, 0)
                prepare(edges, 2, later=True)
                if not first:
                    scale(2 * it - 1)
                center(2 * it)
                prepare_rest(edges, 2)
                finish(edges, 1)
                prepare(edges, 3)
                finish(edges, 2)
                look_up(it + 1)
                prepare(edges, 4, later=True)
                scale(2 * it)
                center(2 * it + 1)
                prepare_rest(edges, 4)
                finish(edges, 3)
                prepare_next(RING * it + RING + 1)

            kv_iteration(0, True)
            with dve.Fori(1, NKV // 2) as it:
                kv_iteration(it)
            scale(NKV - 1)
            dve.wait_ge(S["kvs"], NKV + 2)
            own.step(V.tensor_copy(base_s[:, :], eoff_s[:, :]))
            for c, bank in enumerate((p_y, p_c)):
                last = V.scalar_tensor_tensor(out=kv_s[:, c, :], in0=bank[:, 0, :], scalar=1.0 / NODES,
                                              in1=hmask_s[:, c, :], op0=ALU.mult, op1=ALU.mult)
            last.then_inc(S["kvm"], 1)
            at = p_t[:, :, :].rearrange("p (c a) b -> p c (a b)", c=KD)
            dve.wait_ge(S["at"], 1)
            for c, a in enumerate((mean_s, t1_s)):
                o = 1 - c
                last = V.tensor_copy(a[:, o * P:(o + 1) * P], at[:, c, o * P:(o + 1) * P])
                last = V.tensor_tensor(a[:, c * P:(c + 1) * P], at[:, c, c * P:(c + 1) * P], id_s[:, :], ALU.add)
            last.then_inc(S["atc"], 1)
            dve.wait_ge(S["m1"], 1)
            V.tensor_copy(m1_s[:, :, :], p_h[0][:, :, :].rearrange("p (c a) b -> p c (a b)", c=2))
            V.tensor_tensor(c1_s[:, :], p_h[1][:, 1, 0:2], b1_s[:, :], ALU.add).then_inc(S["c1"], 1)

            def mean(p, edges):
                dve.wait_ge(S["added"], NG + 1 if edges is None else RING * edges[0] + 1)
                own.step(V.tensor_scalar(c_s[:, 0:1], agg_s[:, ds(p, 1), D:D + 1].squeeze(1), 1.0, None, ALU.max))
                own.step(V.reciprocal(c_s[:, 1:2], c_s[:, 0:1]))
                V.tensor_scalar(mean_s[:, :], agg_s[:, ds(p, 1), 0:D].squeeze(1), c_s[:, 1:2], None, ALU.mult
                                ).then_inc(S["mean"], 1)

            def choose(p):
                dve.wait_ge(S["lg"], p)
                own.step(V.tensor_copy(rt_s[:, 1, :], p_c[:, 0, 0:E]), True)
                own.step(V.max(rt_s[:, 2, :], rt_s[:, 1, :]), True)
                own.step(V.max_index(ri_s[:, :], rt_s[:, 2, :], rt_s[:, 1, :]))
                dve.wait_ge(S["ex"], p)
                V.tensor_tensor(rv_s[:, 0:1], rt_s[:, 2, 1:2], rt_s[:, 2, 0:1], ALU.subtract).then_inc(S["mx"], 1)
                own.step(V.tensor_copy(rv_s[:, 6:8], ri_s[:, 0:2]))
                own.step(V.tensor_tensor(oh_s[:, :, :], iota_s[:, 0:E].unsqueeze(1).to_broadcast([P, TOPK, E]),
                                         rv_s[:, 6:8].unsqueeze(2).to_broadcast([P, TOPK, E]), ALU.is_equal))
                V.tensor_tensor(sel_s[:, :], oh_s[:, 0, :], oh_s[:, 1, :], ALU.add).then_inc(S["sel"], 1)

            def position(p):
                dve.wait_ge(S["cnt"], p)
                own.step(V.tensor_tensor(rt_s[:, 3, :], p_c[:, 0, E:2 * E], base_s[:, :], ALU.add))
                V.tensor_tensor(base_s[:, :], p_c[:, 0, 2 * E:3 * E], base_s[:, :], ALU.add).then_inc(S["pos"], 1)
                own.step(V.tensor_tensor(ohp_s[:, :, :], oh_s[:, :, :],
                                         rt_s[:, 3, :].unsqueeze(1).to_broadcast([P, TOPK, E]), ALU.mult))
                own.step(V.tensor_reduce(rv_s[:, 8:10], ohp_s[:, :, :], AX, ALU.add))

            def payload(p):
                dve.wait_ge(S["ex"], p + 1)
                own.step(V.tensor_scalar(rv_s[:, 4:5], rv_s[:, 1:2], 1.0, None, ALU.add))
                own.step(V.reciprocal(rv_s[:, 5:6], rv_s[:, 4:5]))
                dve.wait_ge(S["sc"], 32 * p)
                V.tensor_copy(posi_s[:, :], rv_s[:, 8:10])
                V.tensor_scalar(pay_s[:, :, 0], tcol_s[:, NT:NT + 1].to_broadcast([P, TOPK]),
                                tcol_s[:, ds(p - 1, 1)], None, ALU.add)
                V.tensor_copy(pay_s[:, 0, 1:2].bitcast(F32), rv_s[:, 5:6])
                V.tensor_tensor(pay_s[:, 1, 1:2].bitcast(F32), rv_s[:, 5:6], rv_s[:, 1:2], ALU.mult
                                ).then_inc(S["pay"], 1)

            def gnn_mix(p):
                dve.wait_ge(S["xr"], 16 * p + 16)
                dve.wait_ge(S["xnr"], 16 * p + 16)
                own.step(V.tensor_tensor(t3_s[:, :], xnr_s[:, :], b2_s[:, :], ALU.add))
                dve.wait_ge(S["mix2"], p + 2)
                V.tensor_tensor(t4_s[:, :], p_mix, t3_s[:, :], ALU.add)
                own.step(V.tensor_tensor(t1_s[:, :], p_gnn, xnr_s[:, :], ALU.add))
                own.step(V.scalar_tensor_tensor(out=t2_s[:, :], in0=t1_s[:, :], scalar=0.0, in1=xr_s[:, :],
                                                op0=ALU.max, op1=ALU.add))

            def shared_out(p):
                own.step(V.tensor_tensor(t3_s[:, :], x2_s[:, :], b2s_s[:, :], ALU.add))
                dve.wait_ge(S["y"], p + 1)
                dve.wait_ge(S["ost"], 16 * p)
                V.tensor_tensor(o_s[:, :], p_y[:, 0, :], t3_s[:, :], ALU.add).then_inc(S["o"], 1)

            def normalise(p):
                V.tensor_tensor(x2_s[:, :], t2_s[:, :], t4_s[:, :], ALU.add).then_inc(S["x2"], 1)
                dve.wait_ge(S["const"], 3)
                dve.wait_ge(S["x2"], p + 2)
                own.step(V.bn_stats(st_s[:, 0, :], x2_s[:, :]), True)
                own.step(V.bn_aggr(mv_s[:, 0, :], st_s[:, 0, :]))
                V.tensor_scalar(ve_s[:, 0:1], mv_s[:, 0, 1:2], EPS, None, ALU.add).then_inc(S["ve2"], 1)
                dve.wait_ge(S["sd2"], p + 1)
                own.step(V.reciprocal(rs_s[:, 0:1], sd_s[:, 0:1]))
                dve.wait_ge(S["xfst"], 16 * p + 16)
                V.tensor_scalar(xf_s[:, :], x2_s[:, :], mv_s[:, 0, 0:1], rs_s[:, 0:1], ALU.subtract, ALU.mult
                                ).then_inc(S["xf"], 1)

            def step(p, edges, first=True, second=True):
                summing = edges is not None
                if summing:
                    prepare(edges, 1)
                    finish(edges, 0)
                    prepare(edges, 2, later=True)
                if first:
                    mean(p, edges)
                if summing:
                    prepare_rest(edges, 2)
                if second:
                    choose(p)
                if summing:
                    finish(edges, 1)
                if second:
                    position(p)
                if summing:
                    prepare(edges, 3)
                    finish(edges, 2)
                    look_up(edges[0] + 1)
                    prepare(edges, 4, later=True)
                if first:
                    gnn_mix(p)
                if second:
                    shared_out(p)
                if first:
                    normalise(p)
                if summing:
                    prepare_rest(edges, 4)
                    finish(edges, 3)
                    prepare_next(RING * edges[0] + RING + 1)
                if second:
                    payload(p)

            def plain(edges):
                prepare(edges, 1)
                for b in range(RING):
                    finish(edges, b)
                    if b + 2 <= RING:
                        prepare(edges, b + 2)
                    if b == 1:
                        look_up(edges[0] + 1)
                prepare_next(RING * edges[0] + RING + 1)

            dve.sem_inc(S["ex"], 1)
            node_steps(dve, begin, step, plain)
            own.step(V.tensor_tensor(ntf_s[:, 0, :], base_s[0:1, :], eoff_s[0:1, :], ALU.subtract))
            own.step(V.tensor_scalar(nti_s[:, 0, :], ntf_s[:, 0, :], float(P - 1), None, ALU.add))
            own.step(V.tensor_scalar(nti_s[:, 1, :], nti_s[:, 0, :], 7, None, ALU.arith_shift_right))
            own.step(V.tensor_copy(ntf_s[:, 1, :], nti_s[:, 1, :]))
            own.step(V.memset(ntf_s[:, 2, :], 1.0))
            own.step(V.tensor_tensor_scan(out=ntf_s[:, 3, :], data0=ntf_s[:, 2, :], data1=ntf_s[:, 1, :],
                                          initial=0.0, op0=ALU.mult, op1=ALU.add))
            own.step(V.memset(tabf_s[:, :, :], 0.0))
            step_no = iota_s[0:1, 0:P]
            for e in range(E - 1):
                end = ntf_s[:, 3, e:e + 1]
                own.step(V.tensor_scalar(tabf_s[:, 2, :], step_no, end, ntf_s[:, 1, e:e + 1], ALU.is_ge, ALU.mult))
                own.step(V.tensor_tensor(tabf_s[:, 1, :], tabf_s[:, 1, :], tabf_s[:, 2, :], ALU.add))
                own.step(V.scalar_tensor_tensor(out=tabf_s[:, 3, :], in0=step_no, scalar=end,
                                                in1=tabf_s[:, 0, :], op0=ALU.is_ge, op1=ALU.add))
                own.step(V.tensor_copy(tabf_s[:, 0, :], tabf_s[:, 3, :]))
            own.step(V.tensor_tensor(tabf_s[:, 2, :], step_no, tabf_s[:, 1, :], ALU.subtract))
            own.step(V.tensor_scalar(tabf_s[:, 2, :], tabf_s[:, 2, :], float(P), None, ALU.mult))
            own.step(V.tensor_copy(tabi_s[:, 0, :], tabf_s[:, 0, :]))
            V.tensor_tensor(tabi_s[:, 2, AHEAD:P], tabf_s[:, 0, AHEAD:P], tabf_s[:, 0, 0:P - AHEAD], ALU.is_equal)
            V.scalar_tensor_tensor(out=tabi_s[:, 1, :], in0=tabf_s[:, 0, :], scalar=float(NP),
                                   in1=tabf_s[:, 2, :], op0=ALU.mult, op1=ALU.add).then_inc(S["tab"], 1)

            def tokens(h, s):
                V.tensor_copy(gtok_s[h][:, :], slots_s[:, ds(s, 1), 0:1].squeeze(1)).then_inc(S[f"gtok{h}"], 1)

            def biases(h, s):
                e = dve.value_load(tabi_s[0:1, 0, ds(s, 1)], min_val=0, max_val=E - 1)
                own.step(V.tensor_copy(gate_s[h][:, :], slots_s[:, ds(s, 1), 1:2].squeeze(1).bitcast(F32)), True)
                own.step(V.tensor_scalar(gb2_s[h], b2p_s[:, ds(e, 1), :].squeeze(1), gate_s[h][:, :], None, ALU.mult),
                         True)
                V.tensor_copy(b1_h[h][:, :], b1p_s[:, ds(e, 1), :].squeeze(1)).then_inc(S[f"bias{h}"], 1)

            dve.wait_ge(S["tab"], 1)
            dve.wait_ge(S["bp"], 32)
            for h in range(2):
                dve.wait_ge(S[f"slots{h}"], 16)
            for h in range(2):
                tokens(h, h)
            for h in range(2):
                biases(h, h)
            with dve.Fori(0, STEPS // 2) as it:
                for h in range(2):
                    s = 2 * it + h
                    dve.wait_ge(S["const"], 3)
                    dve.wait_ge(S[f"slots{h}"], 16 * it + 32)
                    dve.wait_ge(S[f"xg{h}"], 16 * it + 16)
                    tokens(h, s + AHEAD)
                    dve.wait_ge(S["const"], 3)
                    dve.wait_ge(S["scat"], 16 * s + 16)
                    own.step(V.tensor_copy(stok_s[h][:, :], slots_s[:, ds(s, 1), 0:1].squeeze(1)))
                    dve.wait_ge(S["yy"], s + 1)
                    V.scalar_tensor_tensor(out=yg_s[h][:, :], in0=y_bank[h], scalar=gate_s[h][:, :], in1=gb2_s[h],
                                           op0=ALU.mult, op1=ALU.add).then_inc(S[f"yg{h}"], 1)
                    dve.wait_ge(S["const"], 3)
                    dve.wait_ge(S[f"yg{h}"], it + 2)
                    biases(h, s + AHEAD)

        @block.tensor
        def _(pe):
            mm = nc.tensor.matmul
            pe.wait_ge(S["wts"], WTS)
            pe.wait_ge(S["const"], 3)
            pe.wait_ge(S["span"], 2)
            for n in ("kvt", "proj", "kvs"):
                pe.sem_inc(S[n], 1)
            pe.sem_inc(S["pass_"], RING)
            xq = pe.alloc_register("extra_pe")
            pe.reg_mov(xq, 1)
            wide = pe.alloc_register("wide_pe")

            def sums(b):
                for u in range(U):
                    m = mm(p_agg[b % 2], onehot[:, b % 2, u, :], ring[b][:, u, :], start=u == 0, stop=u == U - 1)
                return m

            word = Word(pe, word_s[0:1, 0, :], WIDE * NT - 1)

            def begin(it):
                bits = word.now()
                return it, bits >> RING, bits

            def aggregate(edges, b):
                it, _, bits = edges
                g = RING * it + b
                pe.reg_mov(wide, (bits >> b) & 1)
                for u in range(U):
                    pe.wait_ge(s_row[b][u], 16 * it + 16)
                with pe.If_eq(wide, 1):
                    hi = pe.value_load(span_s[0:1, ds(g, 1)], min_val=0, max_val=NT - 1)
                    lo = pe.value_load(span_s[0:1, ds(g + NS, 1)], min_val=0, max_val=NT - 1)
                    with pe.Fori(lo, hi):
                        pe.wait_ge(S["const"], 3)
                        pe.wait_ge(S["xoneh"], xq)
                        sums(b).then_inc(S["xpass"], 1)
                        pe.reg_add(xq, xq, 1)
                pe.wait_ge(S["oneh"], g + 1)
                sums(b).then_inc(S["pass_"], 1)
                if b == 0:
                    word.look_up(it + 1)

            def transpose(to, of):
                return nc.tensor.transpose(to, of, id_s[:, :])

            def project(m, h, it):
                pe.wait_ge(S[f"kvx{h}"], 16 * it + 16)
                pe.wait_ge(S["kvtc"], m + 1)
                for k in range(KD):
                    t = transpose(p_t[:, k, :], kvx_s[h][:, k * P:(k + 1) * P])
                t.then_inc(S["kvt"], 1)
                pe.wait_ge(S["kvtc"], m + 2)
                pe.wait_ge(S["cen"], m + 1)
                for k in range(KD):
                    mm(p_kv, xt_s[:, k, :], wkv_s[:, k, :], start=k == 0, stop=False)
                mm(p_kv, ones_s[0:1, :], bkv_s[:, :], start=False, stop=True).then_inc(S["proj"], 1)

            def k_v(m):
                pe.wait_ge(S["kvh"], m + 1)
                for c, bank in enumerate((p_y, p_c)):
                    t = mm(bank[:, 0, :], kvh_s[:, c * P:(c + 1) * P], kvh_s[:, D:], start=False, stop=False,
                           skip_group_check=True)
                t.then_inc(S["kvs"], 1)

            for bank in (p_y, p_c):
                mm(bank[:, 0, :], zero_s[:, 0:P], zero_s[:, :], start=True, stop=False, skip_group_check=True)

            def kv_iteration(it, first=False):
                edges = begin(it)
                aggregate(edges, 0)
                project(2 * it, 0, it)
                aggregate(edges, 1)
                if not first:
                    k_v(2 * it - 1)
                aggregate(edges, 2)
                project(2 * it + 1, 1, it)
                aggregate(edges, 3)
                k_v(2 * it)

            word.look_up(0)
            kv_iteration(0, True)
            with pe.Fori(1, NKV // 2) as it:
                kv_iteration(it)
            k_v(NKV - 1)
            for bank in (p_y, p_c):
                m = mm(bank[:, 0, :], zero_s[:, 0:P], zero_s[:, :], start=False, stop=True, skip_group_check=True)
            m.then_inc(S["kvs"], 1)
            pe.wait_ge(S["kvm"], 1)
            for c in range(KD):
                for k in range(KD):
                    m = mm(p_t[:, 2 * c:2 * c + 2, :].rearrange("p a b -> p (a b)"), kv_s[:, k, c * P:(c + 1) * P], wq_s[:, k, :], start=k == 0, stop=k == KD - 1)
            m.then_inc(S["at"], 1)
            for c in range(KD):
                for k in range(KD):
                    m = mm(p_h[1][:, 0, c:c + 1], kv_s[:, k, c * P:(c + 1) * P], bq_s[:, k:k + 1],
                           start=k == 0, stop=k == KD - 1)
            m.then_inc(S["bqk"], 1)
            pe.wait_ge(S["atc"], 1)
            at = (mean_s, t1_s)
            for c in range(KD):
                for k in range(KD):
                    mm(p_h[0][:, 2 * c:2 * c + 2, :].rearrange("p a b -> p (a b)"), at[k][:, c * P:(c + 1) * P], w1_s[:, k, :],
                       start=k == 0, stop=k == KD - 1)
            pe.wait_ge(S["bqc"], 1)
            for c in range(KD):
                for k in range(KD):
                    m = mm(p_h[1][:, 1, c:c + 1], w1_s[:, k, c * P:(c + 1) * P], c_s[:, k:k + 1],
                           start=k == 0, stop=k == KD - 1)
            m.then_inc(S["m1"], 1)

            for n in ("mix2", "y"):
                pe.sem_inc(S[n], 1)
            pe.sem_inc(S["h"], KF)
            pe.wait_ge(S["c1"], 1)

            def transpose_xf(p):
                pe.wait_ge(S["xf"], p)
                pe.wait_ge(S["gl"], p * KF + 1)
                for k in range(KD):
                    m = transpose(p_h[1][:, 2 + k, :], xf_s[:, k * P:(k + 1) * P])
                m.then_inc(S["txf"], 1)

            def transpose_xn_mean(p):
                pe.wait_ge(S["xnr"], 16 * p + 16)
                pe.wait_ge(S["mean"], p + 1)
                pe.wait_ge(S["tc"], p + 1)
                for k in range(KD):
                    transpose(p_t[:, k, :], xnr_s[:, k * P:(k + 1) * P])
                for k in range(KD):
                    m = transpose(p_t[:, 2 + k, :], mean_s[:, k * P:(k + 1) * P])
                m.then_inc(S["tm"], 1)

            def logits(p):
                pe.wait_ge(S["xfc"], p)
                pe.wait_ge(S["pos"], p)
                for k in range(KD):
                    m = mm(p_c[:, 0, 0:E], xft_s[:, k, :], wrt_s[:, k, :], start=k == 0, stop=k == KD - 1)
                m.then_inc(S["lg"], 1)

            def sage(p):
                pe.wait_ge(S["tc"], p + 2)
                pe.wait_ge(S["x2"], p + 1)
                for j in range(KD):
                    for k in range(KD):
                        mm(p_a[:, j, :], wl_s[:, k, j * P:(j + 1) * P], xt_s[:, 2 + k, :], start=k == 0, stop=False)
                    for k in range(KD):
                        m = mm(p_a[:, j, :], wr_s[:, k, j * P:(j + 1) * P], xt_s[:, k, :], start=False, stop=k == KD - 1)
                m.then_inc(S["sage"], 1)

            def mix_hidden(p, second):
                if second:
                    pe.wait_ge(S["pos"], p + 1)
                for j in range(KD):
                    for k in range(KD):
                        m = mm(p_c[:, 1, j * P:(j + 1) * P], m1_s[:, k, j * P:(j + 1) * P], xt_s[:, k, :],
                               start=k == 0, stop=k == KD - 1)
                m.then_inc(S["mix1"], 1)

            def gnn(p):
                pe.wait_ge(S["relu"], p + 2)
                for j in range(KD):
                    mm(p_gnn, act_s[:, j, :], wln_s[:, j, :], start=j == 0, stop=j == KD - 1)

            def mix(p):
                pe.wait_ge(S["g1"], p + 2)
                for j in range(KD):
                    m = mm(p_mix, act_s[:, 2 + j, :], w2_s[:, j, :], start=j == 0, stop=j == KD - 1)
                m.then_inc(S["mix2"], 1)

            def shared_up(p, j):
                if j >= 2:
                    pe.wait_ge(S["gl"], p * KF + j)
                for k in range(KD):
                    m = mm(p_h[(j + 1) % 2][:, 0, :], w1s_s[:, k, j * P:(j + 1) * P], xft_s[:, k, :],
                           start=k == 0, stop=k == KD - 1)
                m.then_inc(S["h"], 1)

            def shared_down(p, j):
                pe.wait_ge(S["gl"], p * KF + j + 2)
                m = mm(p_y[:, 0, :], hid_s[:, j, :], w2s_s[:, j, :], start=j == 0, stop=j == KF - 1)
                if j == KF - 1:
                    m.then_inc(S["y"], 1)

            def step(p, edges, first=True, second=True):
                def sum_group(b):
                    if edges is not None:
                        aggregate(edges, b)

                sum_group(0)
                if second:
                    transpose_xf(p)
                sum_group(1)
                if second:
                    logits(p)
                    shared_up(p, 0)
                    shared_up(p, 1)
                sum_group(2)
                if first:
                    transpose_xn_mean(p)
                if second:
                    pe.wait_ge(S["sel"], p)
                    mm(p_c[:, 0, E:2 * E], triu_s[:, :], sel_s[:, :], start=True, stop=True)
                    mm(p_c[:, 0, 2 * E:3 * E], ones_s[:, :], sel_s[:, :], start=True, stop=True
                       ).then_inc(S["cnt"], 1)
                    pe.wait_ge(S["o"], p)
                for j in range(KF):
                    if second:
                        shared_down(p, j)
                        if j + 2 < KF:
                            shared_up(p, j + 2)
                    if j == 1 and first:
                        sage(p)
                    if j == 2 and first:
                        mix_hidden(p, second)
                    if j == 3 and first:
                        gnn(p)
                    if j == 4 and first:
                        mix(p)
                sum_group(3)

            def plain(edges):
                for b in range(RING):
                    aggregate(edges, b)

            node_steps(pe, begin, step, plain)
            pe.wait_ge(S["w2p"], 16)
            pe.wait_ge(S["tab"], 1)

            def transposes(s, h, n):
                pe.wait_ge(S[f"xg{h}"], 16 * n)
                for k in range(KD):
                    m = transpose(p_t[:, k, :], xg_s[h][:, k * P:(k + 1) * P])
                m.then_inc(S["yt"], 1)

            def up(s, h, j):
                pe.wait_ge(S["ygl"], s * KF + j + 1)
                for k in range(KD):
                    m = mm(p_h[j % 2][:, 0, :], w1p_s[h][:, k, j * P:(j + 1) * P], yxt_s[h][:, k, :],
                           start=k == 0, stop=k == KD - 1)
                m.then_inc(S["yh"], 1)

            def ready(s, h, n):
                pe.wait_ge(S["ytc"], s + 1)
                pe.wait_ge(S[f"w1p{h}"], 16 * n)

            transposes(0, 0, 1)
            ready(0, 0, 1)
            up(0, 0, 0)
            up(0, 0, 1)
            with pe.Fori(0, STEPS // 2) as it:
                for h in range(2):
                    s = 2 * it + h
                    e = pe.value_load(tabi_s[0:1, 0, ds(s, 1)], min_val=0, max_val=E - 1)
                    pe.wait_ge(S[f"yg{h}"], it + 1)
                    for j in range(KF):
                        pe.wait_ge(S["ygl"], s * KF + j + 3)
                        m = mm(y_bank[h], hid_s[:, j, :], w2p_s[:, ds(e, 1), j, :].squeeze(1),
                               start=j == 0, stop=j == KF - 1)
                        if j == KF - 1:
                            m.then_inc(S["yy"], 1)
                        if j + 2 == KF:
                            ready(s + 1, 1 - h, it + 1 + h)
                        if j + 2 < KF:
                            up(s, h, j + 2)
                        else:
                            up(s + 1, 1 - h, j + 2 - KF)
                        if j == KF // 2 - 1:
                            transposes(s + 1, 1 - h, it + 1 + h)


_WEIGHTS = ["wl", "bl", "wr", "wln", "wkv", "bkv", "wq", "bq", "kvg", "kvb", "w1", "b1", "w2", "b2", "wrt",
            "w1s", "b1s", "w2s", "b2s", "w1p", "b1p", "w2p", "b2p"]
_CONSTS = ["ident", "triu", "valid", "iota", "tcol", "eoff", "hmask", "slot0"]


def kernel(**inputs):
    import numpy as np
    import concourse.bacc as bacc
    from concourse.bass_utils import run_bass_kernel_spmd as run

    v = {k: np.asarray(a) for k, a in inputs.items()}

    def by_rows(w):
        return w.reshape(w.shape[0] // P, P, -1).transpose(1, 0, 2)

    def column(b):
        return b.reshape(-1, P).T

    def wide(b):
        return np.broadcast_to(b.reshape(1, -1), (P, b.size))

    qkv = v["L0_mix_w_qkv"].reshape(D, HEADS, 3, HC)
    bqkv = v["L0_mix_b_qkv"].reshape(HEADS, 3, HC)
    x = np.zeros((NP, D), np.float32)
    x[:NODES] = v["x"]
    src = np.zeros((NG + RING) * U * P, np.int32)
    src[:EDGES] = v["src"]
    dst = np.full((NG + 2) * U * P, NP - 1, np.int32)
    dst[:EDGES] = v["dst"]
    slot0 = np.zeros((SLOTS, 2), np.int32)
    slot0[:, 0] = NP + np.arange(SLOTS) % P
    a = {
        "x": x,
        "idx": src.reshape(NG + RING, U, P).transpose(0, 2, 1),
        "dst": dst.reshape((NG + 2) * U, P).T,
        "wl": by_rows(v["L0_gnn_W_l"].T), "bl": column(v["L0_gnn_b_l"]),
        "wr": by_rows(v["L0_gnn_W_r"].T), "wln": by_rows(v["L0_gnn_W_ln"].T),
        "wkv": by_rows(np.concatenate([qkv[:, :, 1].reshape(D, D), qkv[:, :, 2].reshape(D, D)], 1)),
        "bkv": np.concatenate([bqkv[:, 1].reshape(1, D), bqkv[:, 2].reshape(1, D)], 1),
        "wq": by_rows(qkv[:, :, 0].reshape(D, D).T), "bq": column(bqkv[:, 0].reshape(D)),
        "kvg": wide(np.concatenate([v["L0_mix_kln_g"], v["L0_mix_vln_g"]])),
        "kvb": wide(np.concatenate([v["L0_mix_kln_b"], v["L0_mix_vln_b"]])),
        "w1": by_rows(v["L0_mix_w1"]), "b1": column(v["L0_mix_b1"]),
        "w2": by_rows(v["L0_mix_w2"]), "b2": wide(v["L0_mix_b2"]),
        "wrt": by_rows(v["L0_ffn_Wr"]),
        "w1s": by_rows(v["L0_ffn_W1s"]), "b1s": column(v["L0_ffn_b1s"]),
        "w2s": by_rows(v["L0_ffn_W2s"]), "b2s": wide(v["L0_ffn_b2s"]),
        "w1p": v["L0_ffn_W1p"], "b1p": v["L0_ffn_b1p"].reshape(E, KF, P).transpose(0, 2, 1),
        "w2p": v["L0_ffn_W2p"], "b2p": v["L0_ffn_b2p"],
        "ident": np.eye(P, dtype=np.float32),
        "triu": np.triu(np.ones((P, P), np.float32), 1),
        "valid": (np.arange(NKV * P).reshape(NKV, P).T < NODES).astype(np.float32),
        "iota": np.broadcast_to(np.arange(P, dtype=np.float32), (P, P)),
        "tcol": np.concatenate([np.broadcast_to(P * np.arange(NT, dtype=np.float32), (P, NT)),
                                np.arange(P, dtype=np.float32)[:, None]], 1),
        "eoff": np.broadcast_to(NP * np.arange(E, dtype=np.float32), (P, E)),
        "hmask": by_rows(np.kron(np.eye(HEADS, dtype=np.float32), np.ones((HC, HC), np.float32))),
        "slot0": slot0,
    }
    nc = bacc.Bacc("TRN2", target_bir_lowering=False, num_devices=1)
    arrays, args = {}, {}
    for name in ["x", "idx", "dst"] + _WEIGHTS + _CONSTS:
        arr = np.ascontiguousarray(a[name])
        arrays[f"in_{name}"] = arr
        args[name] = nc.dram_tensor(f"in_{name}", arr.shape, mybir.dt.from_np(arr.dtype), kind="ExternalInput").ap()
    out = nc.dram_tensor("out_rows", (PADROWS, D), F32, kind="ExternalOutput").ap()
    gps_layer(nc, out=out, **args)
    r = run(nc, [arrays], core_ids=[0])
    return r.results[0]["out_rows"][:NODES]
```
